# Optimizing a Trainium2 kernel written in Bass

```python
import numpy as np
import jax
import jax.numpy as jnp

def _softmax(x, axis=-1):
    return jax.nn.softmax(x, axis=axis)

def _gelu(x):
    return jax.nn.gelu(x, approximate=True)

def _silu(x):
    return jax.nn.silu(x)

def _sigmoid(x):
    return jax.nn.sigmoid(x)

def _layernorm(x, axis=-1, eps=1e-05):
    m = jnp.mean(x, axis=axis, keepdims=True)
    v = jnp.var(x, axis=axis, keepdims=True)
    return (x - m) / jnp.sqrt(v + eps)

def _scatter_add(tgt, idx, src, axis=0):
    return tgt.at[idx].add(src)

def _segment_sum(src, seg, n):
    return jax.ops.segment_sum(src, seg, n)
kernel_name = 'mk_prb_d4_jaxref_r8_19a6c1'

def setup_inputs(seed: int=0):
    np.random.seed(seed)
    _w = jnp.asarray

    def _L0_attn_setup():
        import jax, jax.numpy as jnp
        import numpy as np
        from functools import partial
        B, S, D = (8, 256, 128)
        HEADS, DIM_HEAD = (16, 64)
        MAX_ALLOWABLE = 128 * 128 * 8

        def _max_pow2_divides(n):
            i = 1
            while n % 2 == 0:
                i *= 2
                n //= 2
            return i

        def _n_splits(bh, sq, sk):
            dimprod = bh * sq * sk
            true_divisor = dimprod / MAX_ALLOWABLE
            if true_divisor < 1:
                return 1
            if true_divisor >= bh:
                return bh
            nearest_pow2 = 2 ** np.round(np.log2(true_divisor))
            return int(min(_max_pow2_divides(bh), nearest_pow2))

        def _sdp_attention(q, k, v, scale):
            scores = jnp.einsum('bid,bjd->bij', q, k) * scale
            probs = jax.nn.softmax(scores, axis=2)
            return jnp.einsum('bij,bjd->bid', probs, v)

        def _scan_attention(q, k, v, scale, n_splits):
            bh = q.shape[0]
            nq, nk, nv = [h.reshape(n_splits, bh // n_splits, h.shape[-2], h.shape[-1]) for h in (q, k, v)]

            def body(carry, args):
                cq, ck, cv = args
                return (None, _sdp_attention(cq, ck, cv, scale))
            outs = jax.lax.scan(body, None, (nq, nk, nv))[1]
            return outs.reshape(-1, outs.shape[-2], outs.shape[-1])

        def _heads_to_batch(t, heads):
            b, s, d = t.shape
            return t.reshape(b, s, heads, d // heads).transpose(0, 2, 1, 3).reshape(b * heads, s, d // heads)

        def _batch_to_heads(t, heads):
            bh, s, d = t.shape
            return t.reshape(bh // heads, heads, s, d).transpose(0, 2, 1, 3).reshape(bh // heads, s, d * heads)
        key = jax.random.key(seed)
        k1, k2, k3, k4 = jax.random.split(key, 4)
        inner = HEADS * DIM_HEAD
        return {'hidden_states': jax.random.normal(k1, (B, S, D), jnp.float32), 'Wq': jax.random.normal(k2, (D, inner), jnp.float32) * D ** (-0.5), 'Wkv': jax.random.normal(k3, (D, 2 * inner), jnp.float32) * D ** (-0.5), 'Wo': jax.random.normal(k4, (inner, D), jnp.float32) * inner ** (-0.5), 'bo': jnp.zeros((D,), jnp.float32)}
    _L0_attn_in = _L0_attn_setup()

    def _L0_ffn_setup():
        import jax, jax.numpy as jnp
        import numpy as np
        K = 2
        CAP_FACTOR = 1.25
        key = jax.random.key(seed)
        ks = jax.random.split(key, 6)
        B, T, C, H, E = (8, 256, 128, 512, 8)
        return {'x': jax.random.normal(ks[0], (B, T, C), dtype=jnp.float32), 'Wr': jax.random.normal(ks[1], (C, E), dtype=jnp.float32) * 0.02, 'W1': jax.random.normal(ks[2], (E, C, H), dtype=jnp.float32) * 0.02, 'b1': jax.random.normal(ks[3], (E, H), dtype=jnp.float32) * 0.02, 'W2': jax.random.normal(ks[4], (E, H, C), dtype=jnp.float32) * 0.02, 'b2': jax.random.normal(ks[5], (E, C), dtype=jnp.float32) * 0.02}
    _L0_ffn_in = _L0_ffn_setup()

    def _L1_attn_setup():
        import jax, jax.numpy as jnp
        import numpy as np
        B, L, IN_DIM = (4, 256, 128)
        H, D = (16, 64)
        OUT_DIM = 128
        key = jax.random.key(seed)
        k1, k2, k3 = jax.random.split(key, 3)
        inputs = jax.random.normal(k1, (B, L, IN_DIM), dtype=jnp.float32)
        W_qkv = jax.random.normal(k2, (IN_DIM, 3 * H * D), dtype=jnp.float32) * IN_DIM ** (-0.5)
        W_out = jax.random.normal(k3, (H * D, OUT_DIM), dtype=jnp.float32) * (H * D) ** (-0.5)
        return {'inputs': inputs, 'W_qkv': W_qkv, 'W_out': W_out}
    _L1_attn_in = _L1_attn_setup()

    def _L1_ffn_setup():
        import jax, jax.numpy as jnp
        import numpy as np
        B, S, D = (2, 64, 128)
        E, K, I = (16, 8, 128)
        I_SH = 128
        ROUTE_SCALE = 2.826
        key = jax.random.key(seed)
        ks = jax.random.split(key, 8)
        s = 0.02
        return {'x': jax.random.normal(ks[0], (B, S, D), dtype=jnp.float32), 'gate_w': jax.random.normal(ks[1], (E, D), dtype=jnp.float32) * s, 'expert_bias': jnp.zeros((E,), dtype=jnp.float32), 'w_gate': jax.random.normal(ks[2], (E, I, D), dtype=jnp.float32) * s, 'w_up': jax.random.normal(ks[3], (E, I, D), dtype=jnp.float32) * s, 'w_down': jax.random.normal(ks[4], (E, D, I), dtype=jnp.float32) * s, 'shared_gate_w': jax.random.normal(ks[5], (I_SH, D), dtype=jnp.float32) * s, 'shared_up_w': jax.random.normal(ks[6], (I_SH, D), dtype=jnp.float32) * s, 'shared_down_w': jax.random.normal(ks[7], (D, I_SH), dtype=jnp.float32) * s}
    _L1_ffn_in = _L1_ffn_setup()

    def _L2_attn_setup():
        import jax, jax.numpy as jnp
        import numpy as np
        DIM = 128
        SCALE = 1.0 / np.sqrt(DIM)
        key = jax.random.key(seed)
        ks = jax.random.split(key, 7)
        B, S, D = (4, 256, DIM)
        x = jax.random.normal(ks[0], (B, S, D), dtype=jnp.float32)
        init = 1.0 / np.sqrt(D)
        Wq = jax.random.uniform(ks[1], (D, D), jnp.float32, -init, init)
        Wk = jax.random.uniform(ks[2], (D, D), jnp.float32, -init, init)
        Wv = jax.random.uniform(ks[3], (D, D), jnp.float32, -init, init)
        bq = jax.random.uniform(ks[4], (D,), jnp.float32, -init, init)
        bk = jax.random.uniform(ks[5], (D,), jnp.float32, -init, init)
        bv = jax.random.uniform(ks[6], (D,), jnp.float32, -init, init)
        return {'x': x, 'Wq': Wq, 'bq': bq, 'Wk': Wk, 'bk': bk, 'Wv': Wv, 'bv': bv}
    _L2_attn_in = _L2_attn_setup()

    def _L2_ffn_setup():
        import jax, jax.numpy as jnp
        import numpy as np
        DIM = 128
        DEPTH = 6
        HEADS = 16
        DIM_HEAD = 64
        WINDOW = 32
        INNER = HEADS * DIM_HEAD
        DIM_INNER = int(DIM * 4 * 2 / 3)
        QK_SCALE = 8.0

        def shift_tokens(t):
            a, s = jnp.split(t, 2, -1)
            s = jnp.pad(s, ((0, 0), (1, 0), (0, 0)))[:, :-1]
            return jnp.concatenate([a, s], -1)

        def l2norm(t):
            return t / jnp.maximum(jnp.linalg.norm(t, axis=-1, keepdims=True), 1e-12)

        def rotate_half(x):
            x1, x2 = jnp.split(x, 2, -1)
            return jnp.concatenate([-x2, x1], -1)

        def rotary_tables(n):
            half = jnp.arange(0, DIM_HEAD, 2, dtype=jnp.float32)
            inv_freq = 1.0 / 10000.0 ** (half / DIM_HEAD)
            t = jnp.arange(n, dtype=jnp.float32)
            freqs = t[:, None] * inv_freq[None, :]
            freqs = jnp.concatenate([freqs, freqs], -1)
            base_scale = (half + 0.4 * DIM_HEAD) / (1.4 * DIM_HEAD)
            power = (t - n // 2) / (WINDOW // 2)
            scale = base_scale[None, :] ** power[:, None]
            scale = jnp.concatenate([scale, scale], -1)
            return (freqs, scale)

        def local_attention(q, k, v):
            b, h, n, d = q.shape
            w = WINDOW
            nw = n // w
            bq = q.reshape(b, h, nw, w, d)
            bk = k.reshape(b, h, nw, w, d)
            bv = v.reshape(b, h, nw, w, d)

            def look(t):
                p = jnp.pad(t, ((0, 0), (0, 0), (1, 0), (0, 0), (0, 0)))
                return jnp.concatenate([p[:, :, :nw], p[:, :, 1:]], axis=3)
            bk2, bv2 = (look(bk), look(bv))
            seq = jnp.arange(n).reshape(nw, w)
            seq_p = jnp.pad(seq, ((1, 0), (0, 0)), constant_values=-1)
            jt = jnp.concatenate([seq_p[:nw], seq_p[1:]], axis=1)
            it = seq[:, :, None]
            jb = jt[:, None, :]
            mask = (it < jb) | (it > jb + w) | (jb == -1)
            sim = jnp.einsum('bhwie,bhwje->bhwij', bq, bk2) * QK_SCALE
            sim = jnp.where(mask, -jnp.finfo(sim.dtype).max, sim)
            attn = jax.nn.softmax(sim, -1)
            out = jnp.einsum('bhwij,bhwje->bhwie', attn, bv2)
            return out.reshape(b, h, n, d)

        def attn_layer(x, Wqkv, qs, ksc, Wo):
            b, n, _ = x.shape
            qkv = x @ Wqkv
            q, k, v = jnp.split(qkv, 3, -1)
            sh = lambda t: t.reshape(b, n, HEADS, DIM_HEAD).transpose(0, 2, 1, 3)
            q, k, v = (sh(q), sh(k), sh(v))
            q = l2norm(q) * qs
            k = l2norm(k) * ksc
            freqs, scale = rotary_tables(n)
            cos, sin = (jnp.cos(freqs), jnp.sin(freqs))
            q = q * cos * scale + rotate_half(q) * sin * scale
            inv = 1.0 / scale
            k = k * cos * inv + rotate_half(k) * sin * inv
            out = local_attention(q, k, v)
            out = out.transpose(0, 2, 1, 3).reshape(b, n, INNER)
            return out @ Wo

        def ffn_layer(x, g, bln, W1, b1, W2, b2):
            mu = x.mean(-1, keepdims=True)
            var = ((x - mu) ** 2).mean(-1, keepdims=True)
            xn = (x - mu) / jnp.sqrt(var + 1e-05) * g + bln
            hg = xn @ W1 + b1
            a, gate = jnp.split(hg, 2, -1)
            return a * jax.nn.gelu(gate, approximate=False) @ W2 + b2
        key = jax.random.key(seed)
        ks = jax.random.split(key, 8)
        B, N = (2, 256)
        init = lambda k, shape: jax.random.normal(k, shape, jnp.float32) * 0.02
        return {'x': jax.random.normal(ks[0], (B, N, DIM), jnp.float32), 'Wqkv': init(ks[1], (DEPTH, DIM, 3 * INNER)), 'q_scale': jnp.ones((DEPTH, DIM_HEAD), jnp.float32), 'k_scale': jnp.ones((DEPTH, DIM_HEAD), jnp.float32), 'Wo': init(ks[2], (DEPTH, INNER, DIM)), 'ln_g': jnp.ones((DEPTH, DIM), jnp.float32), 'ln_b': jnp.zeros((DEPTH, DIM), jnp.float32), 'W1': init(ks[3], (DEPTH, DIM, 2 * DIM_INNER)), 'b1': jnp.zeros((DEPTH, 2 * DIM_INNER), jnp.float32), 'W2': init(ks[4], (DEPTH, DIM_INNER, DIM)), 'b2': jnp.zeros((DEPTH, DIM), jnp.float32)}
    _L2_ffn_in = _L2_ffn_setup()

    def _L3_attn_setup():
        import jax, jax.numpy as jnp
        import numpy as np
        D_MODEL = 128
        NUM_HEADS = 16
        HEAD_DIM = D_MODEL // NUM_HEADS
        key = jax.random.key(seed)
        ks = jax.random.split(key, 9)
        s = 1.0 / np.sqrt(D_MODEL)
        x = jax.random.normal(ks[0], (2, 256, D_MODEL), dtype=jnp.float32)
        Wq = jax.random.uniform(ks[1], (D_MODEL, D_MODEL), jnp.float32, -s, s)
        bq = jax.random.uniform(ks[2], (D_MODEL,), jnp.float32, -s, s)
        Wk = jax.random.uniform(ks[3], (D_MODEL, D_MODEL), jnp.float32, -s, s)
        bk = jax.random.uniform(ks[4], (D_MODEL,), jnp.float32, -s, s)
        Wv = jax.random.uniform(ks[5], (D_MODEL, D_MODEL), jnp.float32, -s, s)
        bv = jax.random.uniform(ks[6], (D_MODEL,), jnp.float32, -s, s)
        Wo = jax.random.uniform(ks[7], (D_MODEL, D_MODEL), jnp.float32, -s, s)
        bo = jax.random.uniform(ks[8], (D_MODEL,), jnp.float32, -s, s)
        return {'x': x, 'Wq': Wq, 'bq': bq, 'Wk': Wk, 'bk': bk, 'Wv': Wv, 'bv': bv, 'Wo': Wo, 'bo': bo}
    _L3_attn_in = _L3_attn_setup()

    def _L3_ffn_setup():
        import jax, jax.numpy as jnp
        import numpy as np
        B, T, D, FF, E, TOP_K = (8, 256, 128, 512, 8, 2)
        key = jax.random.key(seed)
        kx, kr, k1, k2 = jax.random.split(key, 4)
        x = jax.random.normal(kx, (B, T, D), dtype=jnp.float32)
        Wr = jax.random.normal(kr, (E, D), dtype=jnp.float32) * 0.02
        W1 = jax.random.normal(k1, (E, D, FF), dtype=jnp.float32) * 0.02
        W2 = jax.random.normal(k2, (E, FF, D), dtype=jnp.float32) * 0.02
        return {'x': x, 'Wr': Wr, 'W1': W1, 'W2': W2}
    _L3_ffn_in = _L3_ffn_setup()
    _d = {'L0_attn_hidden_states': _L0_attn_in['hidden_states'], 'L0_attn_Wq': _L0_attn_in['Wq'], 'L0_attn_Wkv': _L0_attn_in['Wkv'], 'L0_attn_Wo': _L0_attn_in['Wo'], 'L0_attn_bo': _L0_attn_in['bo'], 'L0_ffn_Wr': _L0_ffn_in['Wr'], 'L0_ffn_W1': _L0_ffn_in['W1'], 'L0_ffn_b1': _L0_ffn_in['b1'], 'L0_ffn_W2': _L0_ffn_in['W2'], 'L0_ffn_b2': _L0_ffn_in['b2'], 'L1_attn_W_qkv': _L1_attn_in['W_qkv'], 'L1_attn_W_out': _L1_attn_in['W_out'], 'L1_ffn_gate_w': _L1_ffn_in['gate_w'], 'L1_ffn_expert_bias': _L1_ffn_in['expert_bias'], 'L1_ffn_w_gate': _L1_ffn_in['w_gate'], 'L1_ffn_w_up': _L1_ffn_in['w_up'], 'L1_ffn_w_down': _L1_ffn_in['w_down'], 'L1_ffn_shared_gate_w': _L1_ffn_in['shared_gate_w'], 'L1_ffn_shared_up_w': _L1_ffn_in['shared_up_w'], 'L1_ffn_shared_down_w': _L1_ffn_in['shared_down_w'], 'L2_attn_Wq': _L2_attn_in['Wq'], 'L2_attn_bq': _L2_attn_in['bq'], 'L2_attn_Wk': _L2_attn_in['Wk'], 'L2_attn_bk': _L2_attn_in['bk'], 'L2_attn_Wv': _L2_attn_in['Wv'], 'L2_attn_bv': _L2_attn_in['bv'], 'L2_ffn_Wqkv': _L2_ffn_in['Wqkv'], 'L2_ffn_q_scale': _L2_ffn_in['q_scale'], 'L2_ffn_k_scale': _L2_ffn_in['k_scale'], 'L2_ffn_Wo': _L2_ffn_in['Wo'], 'L2_ffn_ln_g': _L2_ffn_in['ln_g'], 'L2_ffn_ln_b': _L2_ffn_in['ln_b'], 'L2_ffn_W1': _L2_ffn_in['W1'], 'L2_ffn_b1': _L2_ffn_in['b1'], 'L2_ffn_W2': _L2_ffn_in['W2'], 'L2_ffn_b2': _L2_ffn_in['b2'], 'L3_attn_Wq': _L3_attn_in['Wq'], 'L3_attn_bq': _L3_attn_in['bq'], 'L3_attn_Wk': _L3_attn_in['Wk'], 'L3_attn_bk': _L3_attn_in['bk'], 'L3_attn_Wv': _L3_attn_in['Wv'], 'L3_attn_bv': _L3_attn_in['bv'], 'L3_attn_Wo': _L3_attn_in['Wo'], 'L3_attn_bo': _L3_attn_in['bo'], 'L3_ffn_Wr': _L3_ffn_in['Wr'], 'L3_ffn_W1': _L3_ffn_in['W1'], 'L3_ffn_W2': _L3_ffn_in['W2']}
    _x0 = _d['L0_attn_hidden_states']
    _d['L0_attn_hidden_states'] = jax.random.normal(jax.random.fold_in(jax.random.key(seed), 1), (16, 256, 128), dtype=_x0.dtype)
    del _x0
    return _d

def reference(L0_attn_hidden_states, L0_attn_Wq, L0_attn_Wkv, L0_attn_Wo, L0_attn_bo, L0_ffn_Wr, L0_ffn_W1, L0_ffn_b1, L0_ffn_W2, L0_ffn_b2, L1_attn_W_qkv, L1_attn_W_out, L1_ffn_gate_w, L1_ffn_expert_bias, L1_ffn_w_gate, L1_ffn_w_up, L1_ffn_w_down, L1_ffn_shared_gate_w, L1_ffn_shared_up_w, L1_ffn_shared_down_w, L2_attn_Wq, L2_attn_bq, L2_attn_Wk, L2_attn_bk, L2_attn_Wv, L2_attn_bv, L2_ffn_Wqkv, L2_ffn_q_scale, L2_ffn_k_scale, L2_ffn_Wo, L2_ffn_ln_g, L2_ffn_ln_b, L2_ffn_W1, L2_ffn_b1, L2_ffn_W2, L2_ffn_b2, L3_attn_Wq, L3_attn_bq, L3_attn_Wk, L3_attn_bk, L3_attn_Wv, L3_attn_bv, L3_attn_Wo, L3_attn_bo, L3_ffn_Wr, L3_ffn_W1, L3_ffn_W2):

    def _L0_attn_ref(hidden_states, Wq, Wkv, Wo, bo):
        import jax, jax.numpy as jnp
        import numpy as np
        from functools import partial
        B, S, D = (8, 256, 128)
        HEADS, DIM_HEAD = (16, 64)
        MAX_ALLOWABLE = 128 * 128 * 8

        def _max_pow2_divides(n):
            i = 1
            while n % 2 == 0:
                i *= 2
                n //= 2
            return i

        def _n_splits(bh, sq, sk):
            dimprod = bh * sq * sk
            true_divisor = dimprod / MAX_ALLOWABLE
            if true_divisor < 1:
                return 1
            if true_divisor >= bh:
                return bh
            nearest_pow2 = 2 ** np.round(np.log2(true_divisor))
            return int(min(_max_pow2_divides(bh), nearest_pow2))

        def _sdp_attention(q, k, v, scale):
            scores = jnp.einsum('bid,bjd->bij', q, k) * scale
            probs = jax.nn.softmax(scores, axis=2)
            return jnp.einsum('bij,bjd->bid', probs, v)

        def _scan_attention(q, k, v, scale, n_splits):
            bh = q.shape[0]
            nq, nk, nv = [h.reshape(n_splits, bh // n_splits, h.shape[-2], h.shape[-1]) for h in (q, k, v)]

            def body(carry, args):
                cq, ck, cv = args
                return (None, _sdp_attention(cq, ck, cv, scale))
            outs = jax.lax.scan(body, None, (nq, nk, nv))[1]
            return outs.reshape(-1, outs.shape[-2], outs.shape[-1])

        def _heads_to_batch(t, heads):
            b, s, d = t.shape
            return t.reshape(b, s, heads, d // heads).transpose(0, 2, 1, 3).reshape(b * heads, s, d // heads)

        def _batch_to_heads(t, heads):
            bh, s, d = t.shape
            return t.reshape(bh // heads, heads, s, d).transpose(0, 2, 1, 3).reshape(bh // heads, s, d * heads)
        scale = DIM_HEAD ** (-0.5)
        q = hidden_states @ Wq
        kv = hidden_states @ Wkv
        k, v = jnp.split(kv, 2, axis=-1)
        q = _heads_to_batch(q, HEADS)
        k = _heads_to_batch(k, HEADS)
        v = _heads_to_batch(v, HEADS)
        n_splits = _n_splits(q.shape[0], q.shape[1], k.shape[1])
        out = _scan_attention(q, k, v, scale, n_splits)
        out = _batch_to_heads(out, HEADS)
        return out @ Wo + bo

    def _L0_ffn_ref(x, Wr, W1, b1, W2, b2):
        import jax, jax.numpy as jnp
        import numpy as np
        K = 2
        CAP_FACTOR = 1.25
        B, T, C = x.shape
        E = Wr.shape[1]
        capacity = int(T / E * CAP_FACTOR)
        probs = jax.nn.softmax(x @ Wr, axis=-1)
        topk_probs, topk_experts = jax.lax.top_k(probs, K)
        S = T * K
        e_flat = topk_experts.reshape(B, S)
        p_flat = topk_probs.reshape(B, S)
        x_rep = jnp.repeat(x, K, axis=1)
        onehot = jax.nn.one_hot(e_flat, E, dtype=jnp.int32)
        pos_all = jnp.cumsum(onehot, axis=1) - onehot
        pos = jnp.take_along_axis(pos_all, e_flat[..., None], axis=-1)[..., 0]
        keep = pos < capacity
        pos_c = jnp.minimum(pos, capacity - 1)
        b_idx = jnp.broadcast_to(jnp.arange(B)[:, None], (B, S))
        buf = jnp.zeros((E, B, capacity, C), dtype=x.dtype)
        buf = buf.at[e_flat, b_idx, pos_c].add(x_rep * keep[..., None].astype(x.dtype))
        h = jax.nn.relu(jnp.einsum('ebnc,ech->ebnh', buf, W1) + b1[:, None, None, :])
        y = jnp.einsum('ebnh,ehc->ebnc', h, W2) + b2[:, None, None, :]
        y_tok = y[e_flat, b_idx, pos_c]
        y_tok = y_tok * keep[..., None].astype(x.dtype) * p_flat[..., None]
        out = y_tok.reshape(B, T, K, C).sum(axis=2)
        return out

    def _L1_attn_ref(inputs, W_qkv, W_out):
        import jax, jax.numpy as jnp
        import numpy as np
        B, L, IN_DIM = (4, 256, 128)
        H, D = (16, 64)
        OUT_DIM = 128
        b, l, _ = inputs.shape
        qkv = inputs @ W_qkv
        q, k, v = jnp.split(qkv, 3, axis=-1)
        q = q.reshape(b, l, H, D)
        k = k.reshape(b, l, H, D)
        v = v.reshape(b, l, H, D)
        score = jnp.einsum('bihd,bjhd->bijh', q, k) / D ** 0.5
        mask = jnp.tril(jnp.ones((l, l), dtype=score.dtype))[None, :, :, None]
        masked_score = score * mask + 1e+30 * (mask - 1.0)
        wmat = jax.nn.softmax(masked_score, axis=2)
        out = jnp.einsum('bijh,bjhd->bihd', wmat, v).reshape(b, l, H * D)
        return out @ W_out

    def _L1_ffn_ref(x, gate_w, expert_bias, w_gate, w_up, w_down, shared_gate_w, shared_up_w, shared_down_w):
        import jax, jax.numpy as jnp
        import numpy as np
        B, S, D = (2, 64, 128)
        E, K, I = (16, 8, 128)
        I_SH = 128
        ROUTE_SCALE = 2.826
        gates = jnp.einsum('bsd,ed->bse', x, gate_w)
        scores = jax.nn.sigmoid(gates.astype(jnp.float32))
        sel_scores = scores + expert_bias
        _, inds = jax.lax.top_k(sel_scores, K)
        selected = jnp.take_along_axis(scores, inds, axis=-1)
        selected = selected / selected.sum(axis=-1, keepdims=True)
        selected = selected * ROUTE_SCALE
        onehot = jax.nn.one_hot(inds, E, dtype=selected.dtype)
        combine = jnp.einsum('bske,bsk->bse', onehot, selected)
        hg = jnp.einsum('bsd,eid->bsei', x, w_gate)
        hu = jnp.einsum('bsd,eid->bsei', x, w_up)
        h = jax.nn.silu(hg) * hu
        ye = jnp.einsum('bsei,edi->bsed', h, w_down)
        y = jnp.einsum('bsed,bse->bsd', ye, combine).astype(x.dtype)
        g = jnp.einsum('bsd,id->bsi', x, shared_gate_w)
        u = jnp.einsum('bsd,id->bsi', x, shared_up_w)
        y = y + jnp.einsum('bsi,di->bsd', jax.nn.silu(g) * u, shared_down_w)
        return y

    def _L2_attn_ref(x, Wq, bq, Wk, bk, Wv, bv):
        import jax, jax.numpy as jnp
        import numpy as np
        DIM = 128
        SCALE = 1.0 / np.sqrt(DIM)
        q = jnp.einsum('bsd,ed->bse', x, Wq) + bq
        k = jnp.einsum('bsd,ed->bse', x, Wk) + bk
        v = jnp.einsum('bsd,ed->bse', x, Wv) + bv
        scores = jnp.einsum('bqd,bkd->bqk', q, k) * SCALE
        S = x.shape[1]
        causal = jnp.tril(jnp.ones((S, S), dtype=bool))
        scores = jnp.where(causal, scores, -jnp.inf)
        attn = jax.nn.softmax(scores, axis=-1)
        out = jnp.einsum('bqk,bkd->bqd', attn, v)
        return out

    def _L2_ffn_ref(x, Wqkv, q_scale, k_scale, Wo, ln_g, ln_b, W1, b1, W2, b2):
        import jax, jax.numpy as jnp
        import numpy as np
        DIM = 128
        DEPTH = 6
        HEADS = 16
        DIM_HEAD = 64
        WINDOW = 32
        INNER = HEADS * DIM_HEAD
        DIM_INNER = int(DIM * 4 * 2 / 3)
        QK_SCALE = 8.0

        def shift_tokens(t):
            a, s = jnp.split(t, 2, -1)
            s = jnp.pad(s, ((0, 0), (1, 0), (0, 0)))[:, :-1]
            return jnp.concatenate([a, s], -1)

        def l2norm(t):
            return t / jnp.maximum(jnp.linalg.norm(t, axis=-1, keepdims=True), 1e-12)

        def rotate_half(x):
            x1, x2 = jnp.split(x, 2, -1)
            return jnp.concatenate([-x2, x1], -1)

        def rotary_tables(n):
            half = jnp.arange(0, DIM_HEAD, 2, dtype=jnp.float32)
            inv_freq = 1.0 / 10000.0 ** (half / DIM_HEAD)
            t = jnp.arange(n, dtype=jnp.float32)
            freqs = t[:, None] * inv_freq[None, :]
            freqs = jnp.concatenate([freqs, freqs], -1)
            base_scale = (half + 0.4 * DIM_HEAD) / (1.4 * DIM_HEAD)
            power = (t - n // 2) / (WINDOW // 2)
            scale = base_scale[None, :] ** power[:, None]
            scale = jnp.concatenate([scale, scale], -1)
            return (freqs, scale)

        def local_attention(q, k, v):
            b, h, n, d = q.shape
            w = WINDOW
            nw = n // w
            bq = q.reshape(b, h, nw, w, d)
            bk = k.reshape(b, h, nw, w, d)
            bv = v.reshape(b, h, nw, w, d)

            def look(t):
                p = jnp.pad(t, ((0, 0), (0, 0), (1, 0), (0, 0), (0, 0)))
                return jnp.concatenate([p[:, :, :nw], p[:, :, 1:]], axis=3)
            bk2, bv2 = (look(bk), look(bv))
            seq = jnp.arange(n).reshape(nw, w)
            seq_p = jnp.pad(seq, ((1, 0), (0, 0)), constant_values=-1)
            jt = jnp.concatenate([seq_p[:nw], seq_p[1:]], axis=1)
            it = seq[:, :, None]
            jb = jt[:, None, :]
            mask = (it < jb) | (it > jb + w) | (jb == -1)
            sim = jnp.einsum('bhwie,bhwje->bhwij', bq, bk2) * QK_SCALE
            sim = jnp.where(mask, -jnp.finfo(sim.dtype).max, sim)
            attn = jax.nn.softmax(sim, -1)
            out = jnp.einsum('bhwij,bhwje->bhwie', attn, bv2)
            return out.reshape(b, h, n, d)

        def attn_layer(x, Wqkv, qs, ksc, Wo):
            b, n, _ = x.shape
            qkv = x @ Wqkv
            q, k, v = jnp.split(qkv, 3, -1)
            sh = lambda t: t.reshape(b, n, HEADS, DIM_HEAD).transpose(0, 2, 1, 3)
            q, k, v = (sh(q), sh(k), sh(v))
            q = l2norm(q) * qs
            k = l2norm(k) * ksc
            freqs, scale = rotary_tables(n)
            cos, sin = (jnp.cos(freqs), jnp.sin(freqs))
            q = q * cos * scale + rotate_half(q) * sin * scale
            inv = 1.0 / scale
            k = k * cos * inv + rotate_half(k) * sin * inv
            out = local_attention(q, k, v)
            out = out.transpose(0, 2, 1, 3).reshape(b, n, INNER)
            return out @ Wo

        def ffn_layer(x, g, bln, W1, b1, W2, b2):
            mu = x.mean(-1, keepdims=True)
            var = ((x - mu) ** 2).mean(-1, keepdims=True)
            xn = (x - mu) / jnp.sqrt(var + 1e-05) * g + bln
            hg = xn @ W1 + b1
            a, gate = jnp.split(hg, 2, -1)
            return a * jax.nn.gelu(gate, approximate=False) @ W2 + b2
        for i in range(DEPTH):
            x = attn_layer(shift_tokens(x), Wqkv[i], q_scale[i], k_scale[i], Wo[i]) + x
            x = ffn_layer(shift_tokens(x), ln_g[i], ln_b[i], W1[i], b1[i], W2[i], b2[i]) + x
        return x

    def _L3_attn_ref(x, Wq, bq, Wk, bk, Wv, bv, Wo, bo):
        import jax, jax.numpy as jnp
        import numpy as np
        D_MODEL = 128
        NUM_HEADS = 16
        HEAD_DIM = D_MODEL // NUM_HEADS
        B, S, D = x.shape
        H, Hd = (NUM_HEADS, HEAD_DIM)

        def proj(W, b):
            y = x @ W + b
            return y.reshape(B, S, H, Hd).transpose(0, 2, 1, 3)
        Q, K, V = (proj(Wq, bq), proj(Wk, bk), proj(Wv, bv))
        scale = 1.0 / np.sqrt(Hd).astype(np.float32)
        scores = jnp.einsum('bhqd,bhkd->bhqk', Q, K) * scale
        attn = jax.nn.softmax(scores, axis=-1)
        out = jnp.einsum('bhqk,bhkd->bhqd', attn, V)
        out = out.transpose(0, 2, 1, 3).reshape(B, S, D)
        return out @ Wo + bo

    def _L3_ffn_ref(x, Wr, W1, W2):
        import jax, jax.numpy as jnp
        import numpy as np
        B, T, D, FF, E, TOP_K = (8, 256, 128, 512, 8, 2)
        Bs, Ts, Ds = x.shape
        Ne = Wr.shape[0]
        xf = x.reshape(-1, Ds)
        N = xf.shape[0]
        logits = xf @ Wr.T
        topk_vals, topk_idx = jax.lax.top_k(logits, TOP_K)
        w = jax.nn.softmax(topk_vals.astype(jnp.float32), axis=-1).astype(x.dtype)
        idx_flat = topk_idx.reshape(-1)
        w_flat = w.reshape(-1)
        sort_idx = jnp.argsort(idx_flat)
        rev = sort_idx // TOP_K
        sw = w_flat[sort_idx]
        perm = xf[rev]
        S = perm.shape[0]
        chunks = perm.reshape(Ne, S // Ne, Ds)
        h = jax.nn.gelu(jnp.einsum('ecd,edf->ecf', chunks, W1), approximate=False)
        eo = jnp.einsum('ecf,efd->ecd', h, W2).reshape(S, Ds)
        out = jnp.zeros((N, Ds), dtype=x.dtype).at[rev].add(eo * sw[:, None])
        return out.reshape(Bs, Ts, Ds)
    x = L0_attn_hidden_states
    xn = _layernorm(x, axis=-1)
    x = x + _L0_attn_ref(xn, L0_attn_Wq, L0_attn_Wkv, L0_attn_Wo, L0_attn_bo) + _L0_ffn_ref(xn, L0_ffn_Wr, L0_ffn_W1, L0_ffn_b1, L0_ffn_W2, L0_ffn_b2)
    xn = _layernorm(x, axis=-1)
    x = x + _L1_attn_ref(xn, L1_attn_W_qkv, L1_attn_W_out) + _L1_ffn_ref(xn, L1_ffn_gate_w, L1_ffn_expert_bias, L1_ffn_w_gate, L1_ffn_w_up, L1_ffn_w_down, L1_ffn_shared_gate_w, L1_ffn_shared_up_w, L1_ffn_shared_down_w)
    xn = _layernorm(x, axis=-1)
    x = x + _L2_attn_ref(xn, L2_attn_Wq, L2_attn_bq, L2_attn_Wk, L2_attn_bk, L2_attn_Wv, L2_attn_bv) + _L2_ffn_ref(xn, L2_ffn_Wqkv, L2_ffn_q_scale, L2_ffn_k_scale, L2_ffn_Wo, L2_ffn_ln_g, L2_ffn_ln_b, L2_ffn_W1, L2_ffn_b1, L2_ffn_W2, L2_ffn_b2)
    xn = _layernorm(x, axis=-1)
    x = x + _L3_attn_ref(xn, L3_attn_Wq, L3_attn_bq, L3_attn_Wk, L3_attn_bk, L3_attn_Wv, L3_attn_bv, L3_attn_Wo, L3_attn_bo) + _L3_ffn_ref(xn, L3_ffn_Wr, L3_ffn_W1, L3_ffn_W2)
    return x

_drawn_inputs = setup_inputs


def setup_inputs(seed=0):
    import zlib

    import numpy as np

    out = dict(_drawn_inputs(seed))
    spreads = {'L0_attn_bo': (0.0, 0.1),
     'L1_ffn_expert_bias': (0.0, 0.8),
     'L2_ffn_q_scale': (1.0, 0.6),
     'L2_ffn_k_scale': (1.0, 0.6),
     'L2_ffn_ln_g': (1.0, 0.6),
     'L2_ffn_ln_b': (0.0, 0.8),
     'L2_ffn_b1': (0.0, 0.8),
     'L2_ffn_b2': (0.0, 0.1)}
    factors = {'L0_ffn_Wr': 4.505,
     'L0_ffn_W1': 5.033,
     'L0_ffn_b1': 8.0,
     'L0_ffn_W2': 3.898,
     'L0_ffn_b2': 8.0,
     'L1_ffn_gate_w': 8.0,
     'L1_ffn_w_gate': 8.0,
     'L1_ffn_w_up': 8.0,
     'L1_ffn_w_down': 8.0,
     'L1_ffn_shared_gate_w': 8.0,
     'L1_ffn_shared_up_w': 8.0,
     'L1_ffn_shared_down_w': 8.0,
     'L2_attn_Wq': 3.916,
     'L2_attn_bq': 25.126,
     'L2_attn_Wk': 3.905,
     'L2_attn_bk': 64.0,
     'L2_ffn_W1': 3.689,
     'L2_ffn_W2': 3.652,
     'L3_attn_Wq': 8.0,
     'L3_attn_bq': 46.372,
     'L3_attn_Wk': 8.0,
     'L3_attn_bk': 64.0,
     'L3_attn_bv': 14.971,
     'L3_ffn_Wr': 3.519,
     'L3_ffn_W1': 3.121,
     'L3_ffn_W2': 3.093,
     'L2_attn_bv': 6.642,
     'L3_attn_bo': 8.0}
    for name, (base, spread) in spreads.items():
        noise = np.random.default_rng([zlib.crc32(name.encode()), seed]).standard_normal(out[name].shape)
        drawn = base * np.exp(spread * noise) if base else spread * noise
        out[name] = jnp.asarray(drawn.astype(out[name].dtype))
    for name, factor in factors.items():
        out[name] = (out[name] * factor).astype(out[name].dtype)
    return out
```

```python
from contextlib import ExitStack, contextmanager

import numpy as np

import concourse.bass as bass
from concourse import mybir

F32 = mybir.dt.float32
BF16 = mybir.dt.bfloat16
ALU = mybir.AluOpType
ACT = mybir.ActivationFunctionType
AX = mybir.AxisListType.X

P = 128
BATCH, SEQ, D = 16, 256, 128
TOKENS = BATCH * SEQ
TILES = TOKENS // P
DEPTH = 6
WINDOW = 32
EPS = 1e-5
NEG = -1e30
BANK = 512
CHUNK = 512
CHUNKS = TOKENS // CHUNK
DMA = 16


class Core:

    def __init__(self, nc, ctx):
        self.nc, self.ctx = nc, ctx
        self.banks = [ctx.enter_context(nc.psum_tensor(f"bank{i}", [P, BANK], F32)) for i in range(8)]

    def keep(self, name, shape, dt=F32):
        return self.ctx.enter_context(self.nc.sbuf_tensor(name, shape, dt))

    def sems(self, stage, *names):
        return [self.nc.alloc_semaphore(f"{stage}_{n}") for n in names]


@contextmanager
def stage(core):
    before = core.nc.snapshot_sems()
    yield
    core.nc.clear_and_free_semaphores(core.nc.allocated_since(before))
    core.nc.all_engine_barrier()


def as_stage(build_stage):
    def wrapped(core, *args, **kwargs):
        with stage(core):
            build_stage(core, *args, **kwargs)

    return wrapped


def chain(eng, sem, base=0):
    done = [0]

    def link(ins):
        done[0] += 1
        ins.then_inc(sem, 1)
        eng.wait_ge(sem, base + done[0])

    return link


def began(count):
    return not isinstance(count, int) or count > 0


def tile_of(n):
    return slice(n * P, (n + 1) * P)


def along(column, n):
    return column.unsqueeze(2).to_broadcast([column.shape[0], column.shape[1], n])


def buffer_of(heads):
    return lambda p, j: (p * heads + j) % 2


@as_stage
def load(core, pairs, masks):
    nc = core.nc
    (loaded,) = core.sems("load", "loaded")
    with nc.Block() as block:
        @block.sync
        def _(sp):
            for dst, src in pairs:
                sp.dma_start(dst, src).then_inc(loaded, DMA)

        @block.vector
        def _(dve):
            dve.wait_ge(loaded, DMA * len(pairs))
            nc.vector.tensor_copy(core.masks[:], masks[:])
            nc.vector.tensor_copy(core.ident_bf[:], core.ident[:])
            nc.vector.memset(core.minus_half[:], -0.5)
            nc.vector.memset(core.ones[:], 1.0)


def add_row(core, name, res, row):
    nc = core.nc
    with nc.Block() as block:
        @block.vector
        def _(dve):
            nc.vector.tensor_tensor(res[:], res[:], row.unsqueeze(1).to_broadcast([P, TILES, D]), ALU.add)


def add_rows(core, res, more):
    nc = core.nc
    with nc.Block() as block:
        @block.vector
        def _(dve):
            nc.vector.tensor_tensor(res[:], res[:], more[:], ALU.add)


@as_stage
def store(core, res, out):
    nc = core.nc
    (stored,) = core.sems("store", "stored")
    with nc.Block() as block:
        @block.sync
        def _(sp):
            sp.dma_start(out.rearrange("b (t p) d -> p (b t) d", p=P), res[:]).then_inc(stored, DMA)
            sp.wait_ge(stored, DMA)


@as_stage
def normalise(core, name, src, dst_t, rows=None, shift=False, norm=True, gain_bias=None, layer=0):
    nc, H, N = core.nc, D // 2, TILES * P // BANK
    copied, zeroed, shifted, chained, centred, squared, var_ready, rstd_ready, rows_ready, in_psum, gains_loaded = core.sems(
        name, "copied", "zeroed", "shifted", "chained", "centred", "squared", "var_ready", "rstd_ready",
        "rows_ready", "in_psum", "gains_loaded")
    with ExitStack() as ctx:
        def sb(n, shape, dt=F32):
            return ctx.enter_context(nc.sbuf_tensor(f"{name}_{n}", shape, dt))

        work = sb("work", [P, TILES, D]) if shift else src
        if norm:
            xc = rows if rows is not None else sb("centred", [P, TILES, D])
            squares = sb("squares", [P, TILES, D])
            mean, var, rstd = (sb(n, [P, TILES]) for n in ("mean", "var", "rstd"))
        final = xc if norm else work
        gains = sb("gains", [P, 2]) if gain_bias is not None else None

        with nc.Block() as block:
            if shift:
                @block.sync
                def _(sp):
                    sp.wait_ge(zeroed, 1)
                    sp.dma_start(work[1:P, :, H:D], src[0:P - 1, :, H:D]).then_inc(shifted, DMA)
                    into = work[0:1, :, H:D].rearrange("p (b t) d -> p b t d", t=2)
                    last = src[P - 1:P, :, H:D].rearrange("p (b t) d -> p b t d", t=2)
                    sp.dma_start(into[:, :, 1, :], last[:, :, 0, :]).then_inc(shifted, DMA)
                    if gain_bias is not None:
                        src_gb = gain_bias[bass.ds(layer, 1), :, :].rearrange("a p n -> p (a n)")
                        sp.dma_start(gains[:], src_gb).then_inc(gains_loaded, DMA)

            @block.vector
            def _(dve):
                link = chain(dve, chained)
                if shift:
                    nc.vector.memset(work[0:1, :, H:D], 0.0).then_inc(zeroed, 1)
                    nc.vector.tensor_copy(work[:, :, 0:H], src[:, :, 0:H]).then_inc(copied, 1)
                    if norm:
                        dve.wait_ge(copied, 1)
                        dve.wait_ge(shifted, 2 * DMA)
                if norm:
                    link(nc.vector.tensor_reduce(mean[:], work[:], AX, ALU.add))
                    link(nc.vector.tensor_scalar(mean[:], mean[:], 1.0 / D, None, ALU.mult))
                    nc.vector.tensor_tensor(xc[:], work[:], along(mean[:], D), ALU.subtract).then_inc(centred, 1)
                    dve.wait_ge(squared, 1)
                    link(nc.vector.tensor_reduce(var[:], squares[:], AX, ALU.add))
                    nc.vector.tensor_scalar(var[:], var[:], 1.0 / D, EPS, ALU.mult, ALU.add).then_inc(var_ready, 1)
                    dve.wait_ge(rstd_ready, 1)
                    nc.vector.tensor_tensor(xc[:], xc[:], along(rstd[:], D), ALU.mult).then_inc(rows_ready, 1)

            if norm:
                @block.gpsimd
                def _(pool):
                    pool.wait_ge(var_ready, 1)
                    nc.gpsimd.tensor_tensor(rstd[:], var[:], core.minus_half[:, 0:TILES], ALU.pow).then_inc(rstd_ready, 1)

            @block.scalar
            def _(act):
                if norm:
                    act.wait_ge(centred, 1)
                    nc.scalar.activation(squares[:], xc[:], ACT.Square).then_inc(squared, 1)
                if gain_bias is not None:
                    act.wait_ge(gains_loaded, DMA)
                for q in range(N):
                    act.wait_ge(in_psum, q + 1)
                    dst = dst_t[:, q * BANK:(q + 1) * BANK]
                    if gain_bias is None:
                        nc.scalar.activation(dst, core.banks[q][:], ACT.Copy)
                    else:
                        nc.scalar.activation(dst, core.banks[q][:], ACT.Identity, scale=gains[:, 0:1],
                                             bias=gains[:, 1:2])

            @block.tensor
            def _(pe):
                if norm:
                    pe.wait_ge(rows_ready, 1)
                elif shift:
                    pe.wait_ge(copied, 1)
                    pe.wait_ge(shifted, 2 * DMA)
                for q in range(N):
                    for i in range(BANK // P):
                        last = nc.tensor.transpose(core.banks[q][:, i * P:(i + 1) * P],
                                                   final[:, BANK // P * q + i, :], core.ident[:])
                    last.then_inc(in_psum, 1)


@as_stage
def attention(core, name, w_dram, src_t, res, groups, heads, causal=False, window=False, scale=None,
              biased=False, rotary=None, layer=0):
    nc, hs, G, NB = core.nc, P // heads, groups, BATCH
    masked = causal or window
    keys = [(0, P), (P - WINDOW, 2 * P)] if window else [(0, P), (0, 2 * P)] if causal else [(0, 2 * P)] * 2
    blocks = [(0, 0), (0, 1), (1, 1)] if masked else [(0, 0), (0, 1), (1, 0), (1, 1)]
    late = P if masked else 0
    halves = min(G, 2)
    w_loads = (G // 2 + 1, max(G // 2, 1))
    ahead = 3 if rotary else 2

    x_loaded = core.sems(name, *(f"x_loaded{i}" for i in range(4)))
    w_loaded = core.sems(name, "w_loaded0", "w_loaded1")
    (qk_projected, v_projected, qk_ready, v_ready, scores_ready, max_ready, exp_done, inverse_ready, probs_ready,
     probs_turned, probs_t_ready, heads_done, heads_ready, out_ready, added) = core.sems(
        name, "qk_projected", "v_projected", "qk_ready", "v_ready", "scores_ready", "max_ready", "exp_done",
        "inverse_ready", "probs_ready", "probs_turned", "probs_t_ready", "heads_done", "heads_ready", "out_ready",
        "added")
    if rotary:
        projected, rows_ready, squares_ready, sums_ready, norms_ready, sin_done, summed, rotated, squares_summed = core.sems(
            name, "projected", "rows_ready", "squares_ready", "sums_ready", "norms_ready", "sin_done", "summed",
            "rotated", "squares_summed")

    with ExitStack() as ctx:
        def sb(n, shape, dt=F32):
            return ctx.enter_context(nc.sbuf_tensor(f"{name}_{n}", shape, dt))

        w = [sb(f"w{i}", [P, w_dram.shape[2]]) for i in range(2)]
        x = [sb(f"x{i}", [P, SEQ]) for i in range(4)]
        qk = [sb(f"qk{i}", [P, 2 * SEQ]) for i in range(2)]
        v = [sb(f"v{i}", [P, 2, P]) for i in range(2)]
        probs = [[sb(f"probs{i}_{j}", [P, 2, SEQ]) for j in range(heads)] for i in range(2)]
        probs_t = [sb(f"probs_t{i}", [P, len(blocks) * P]) for i in range(2)]
        heads_t = sb("heads_t", [P, SEQ])
        neg_max, sums, inverse = (sb(n, [P, heads, 2]) for n in ("neg_max", "sums", "inverse"))
        if rotary:
            cos, sin = rotary
            rows, squares, by_sin, rot = (sb(n, [P, 2, 2 * P]) for n in ("rows", "squares", "by_sin", "rot"))
            by_cos = [sb(f"by_cos{i}", [P, 2, 2 * P]) for i in range(2)]
            square_sums, norms = sb("square_sums", [P, 8]), sb("norms", [P, 8])
            rows_p = core.banks[2]
        qk_p, v_p = core.banks[0], core.banks[1]
        out_p = core.banks[3]
        scores_p, turned_p = core.banks[4:6], core.banks[6:8]

        def schedule(eng, start, item, group=None):
            start()

            def group_pair(gp):
                for half in range(halves):
                    quad = gp * (NB // 2) + half * (NB // 4)
                    if group:
                        group(gp * 2 + half, half, quad * 4)
                    with eng.Fori(0, NB // 4 - 1) as i:
                        for p in range(4):
                            item(quad + i, p, [half] * 4, i * 4 + p, gp)
                    for p in range(4):
                        item(quad + NB // 4 - 1, p, [half if p + n < 4 else 1 - half for n in range(4)], NB - 4 + p, gp)

            if G > 2:
                with eng.Fori(0, G // 2) as gp:
                    group_pair(gp)
            else:
                group_pair(0)

        buffer = buffer_of(heads)

        with nc.Block() as block:
            @block.sync
            def _(sp):
                def load_x(p, b):
                    sp.dma_start(x[p][:], src_t[:, bass.ds(b * SEQ, SEQ)]).then_inc(x_loaded[p], DMA)

                def start():
                    for b in range(4):
                        load_x(b, b)

                def item(quad, p, buffers, b, gp):
                    sp.wait_ge(v_projected, quad * 4 + p + 1)
                    load_x(p, b + 4 if not isinstance(b, int) else (b + 4) % NB)

                schedule(sp, start, item)
                for p in range(4):
                    sp.wait_ge(x_loaded[p], (G * NB // 4 + 1) * DMA)

            @block.gpsimd
            def _(pool):
                def load_w(g, buffer):
                    src = w_dram[bass.ds(layer * G + g, 1), :, :].rearrange("a p n -> p (a n)")
                    pool.dma_start(w[buffer][:], src).then_inc(w_loaded[buffer], DMA)

                def norm_factors(a, p):
                    both = by_cos[p % 2]
                    pool.wait_ge(sums_ready, a + 1)
                    if began(a):
                        pool.wait_ge(rotated, a)
                    nc.gpsimd.tensor_tensor(norms[:], square_sums[:], core.minus_half[:, 0:8], ALU.pow)\
                        .then_inc(norms_ready, 1)
                    pool.wait_ge(sin_done, a + 1)
                    nc.gpsimd.tensor_tensor(both[:], both[:], by_sin[:], ALU.add).then_inc(summed, 1)
                    pool.wait_ge(norms_ready, a + 1)
                    pool.wait_ge(summed, a + 1)
                    pool.wait_ge(qk_projected, a)
                    nc.gpsimd.tensor_tensor(rot[:].rearrange("p t (h d) -> p (t h) d", d=hs),
                                            both[:].rearrange("p t (h d) -> p (t h) d", d=hs),
                                            along(norms[:], hs), ALU.mult).then_inc(rotated, 1)

                def start():
                    load_w(0, 0)
                    if rotary:
                        for a in range(3):
                            norm_factors(a, a)

                def group(g, half, first):
                    pool.wait_ge(out_ready, first + 1)
                    load_w(g + 1, 1 - half)

                def item(quad, p, buffers, b, gp):
                    if rotary:
                        norm_factors(quad * 4 + p + 3, p + 3)

                schedule(pool, start, item, group)
                for buffer in range(2):
                    pool.wait_ge(w_loaded[buffer], w_loads[buffer] * DMA)

            @block.tensor
            def _(pe):
                def project_rows(a, quad, p, wb):
                    pe.wait_ge(x_loaded[p], (quad + 1) * DMA)
                    pe.wait_ge(rows_ready, a)
                    for t in range(2):
                        last = nc.tensor.matmul(rows_p[:, t * 2 * P:(t + 1) * 2 * P], x[p][:, tile_of(t)],
                                                w[wb][:, 0:2 * P], start=True, stop=True)
                    last.then_inc(projected, 1)

                def project_qk(a, quad, p, wb):
                    if rotary:
                        pe.wait_ge(rotated, a + 1)
                        pe.wait_ge(qk_ready, a)
                        for n in range(2):
                            for t in range(2):
                                last = nc.tensor.transpose(qk_p[:, (2 * n + t) * P:(2 * n + t + 1) * P],
                                                           rot[:, t, tile_of(n)], core.ident[:])
                        last.then_inc(qk_projected, 1)
                    else:
                        pe.wait_ge(x_loaded[p], (quad + 1) * DMA)
                        pe.wait_ge(qk_ready, a)
                        for n in range(2):
                            last = nc.tensor.matmul(qk_p[:, n * SEQ:(n + 1) * SEQ], w[wb][:, tile_of(n)], x[p][:],
                                                    start=True, stop=True)
                        last.then_inc(qk_projected, 1)

                def project_v(a, p, wb):
                    pe.wait_ge(v_ready, a)
                    for t in range(2):
                        last = nc.tensor.matmul(v_p[:, tile_of(t)], x[p][:, tile_of(t)], w[wb][:, 2 * P:3 * P],
                                                start=True, stop=True)
                    last.then_inc(v_projected, 1)

                def scores(item_b, item_a, p, j, first=False):
                    if j == 0:
                        pe.wait_ge(qk_ready, item_a + 1)
                    if not first and heads > 1:
                        pe.wait_ge(exp_done, item_b * heads + j - 1)
                    bank = scores_p[buffer(p, j)]
                    of_head = slice(hs * j, hs * (j + 1))
                    for t in range(2):
                        k0, k1 = keys[t]
                        last = nc.tensor.matmul(bank[:, t * SEQ + k0:t * SEQ + k1], qk[p % 2][of_head, tile_of(t)],
                                                qk[p % 2][of_head, SEQ + k0:SEQ + k1], start=True, stop=not masked)
                        if masked:
                            if causal:
                                k0, mask = t * P, core.causal_mask[:]
                            else:
                                mask = core.window_mask[:, 0:P] if t == 0 else core.window_mask[:, P:2 * P + WINDOW]
                            last = nc.tensor.matmul(bank[:, t * SEQ + k0:t * SEQ + k1], core.ident_bf[:], mask,
                                                    start=False, stop=True)
                    last.then_inc(scores_ready, 1)

                def turn(item_c, item_b, p, j):
                    pe.wait_ge(probs_ready, item_b * heads + j + 1)
                    for n, (kt, qt) in enumerate(blocks):
                        last = nc.tensor.transpose(turned_p[buffer(p, j)][:, tile_of(n)], probs[p % 2][j][:, qt, tile_of(kt)],
                                                   core.ident[:])
                    last.then_inc(probs_turned, 1)

                def weigh(item_c, item_a, p, j):
                    if j == 0:
                        pe.wait_ge(v_ready, item_a + 1)
                        pe.wait_ge(added, item_c + 1)
                    pe.wait_ge(probs_t_ready, item_c * heads + j + 1)
                    of_head = slice(hs * j, hs * (j + 1))
                    pt = probs_t[buffer(p, j)]
                    nc.tensor.matmul(out_p[of_head, 0:SEQ], v[p % 2][:, 0, of_head], pt[:, 0:SEQ], start=True, stop=False)
                    last = nc.tensor.matmul(out_p[of_head, late:SEQ], v[p % 2][:, 1, of_head], pt[:, SEQ:], start=False,
                                            stop=True)
                    if j == heads - 1:
                        last.then_inc(heads_done, 1)

                def output(item_c, wb):
                    pe.wait_ge(heads_ready, item_c + 1)
                    for t in range(2):
                        last = nc.tensor.matmul(out_p[:, SEQ + t * P:SEQ + (t + 1) * P], heads_t[:, tile_of(t)],
                                                w[wb][:, 3 * P:4 * P], start=True, stop=True)
                    last.then_inc(out_ready, 1)

                def start():
                    pe.wait_ge(w_loaded[0], DMA)
                    if rotary:
                        project_rows(0, 0, 0, 0)
                        project_rows(1, 0, 1, 0)
                    for a in range(2):
                        project_qk(a, 0, a, 0)
                        project_v(a, a, 0)
                    if rotary:
                        project_rows(2, 0, 2, 0)
                    for j in range(heads):
                        scores(0, 0, 0, j, first=j < 2)

                def item(quad, p, buffers, b, gp):
                    k, now = quad * 4 + p, buffers[0]
                    if now != buffers[ahead] and now == buffers[ahead - 1]:
                        loads = gp + 1 if buffers[ahead] else gp + 2
                        pe.wait_ge(w_loaded[buffers[ahead]], loads * DMA)
                    if rotary:
                        project_rows(k + 3, quad + (p + 3) // 4, (p + 3) % 4, buffers[3])
                    for pass_ in range(0, heads, 2):
                        pass_heads = range(pass_, min(pass_ + 2, heads))
                        for j in pass_heads:
                            turn(k, k, p, j)
                        for j in pass_heads:
                            scores(k + 1, k + 1, p + 1, j)
                        for j in pass_heads:
                            weigh(k, k, p, j)
                    project_qk(k + 2, quad + (p + 2) // 4, (p + 2) % 4, buffers[2])
                    project_v(k + 2, (p + 2) % 4, buffers[2])
                    output(k, now)

                schedule(pe, start, item)

            @block.scalar
            def _(act):
                def copy_qk(a, p):
                    act.wait_ge(qk_projected, a + 1)
                    if rotary:
                        nc.scalar.activation(qk[p % 2][:], qk_p[:], ACT.Copy).then_inc(qk_ready, 1)
                    else:
                        nc.scalar.activation(qk[p % 2][:, 0:SEQ], qk_p[:, 0:SEQ], ACT.Copy, scale=scale)
                        nc.scalar.activation(qk[p % 2][:, SEQ:], qk_p[:, SEQ:], ACT.Copy).then_inc(qk_ready, 1)

                def copy_v(a, p, after_c=None):
                    act.wait_ge(v_projected, a + 1)
                    if after_c is not None:
                        act.wait_ge(heads_done, after_c)
                    nc.scalar.activation(v[p % 2][:], v_p[:, 0:SEQ].rearrange("p (t d) -> p t d", t=2), ACT.Copy)\
                        .then_inc(v_ready, 1)

                def copy_rows(a):
                    act.wait_ge(projected, a + 1)
                    act.wait_ge(sin_done, a)
                    nc.scalar.activation(rows[:], rows_p[:].rearrange("p (t n) -> p t n", t=2), ACT.Copy)\
                        .then_inc(rows_ready, 1)

                def square_rows(a):
                    act.wait_ge(rows_ready, a + 1)
                    if began(a):
                        act.wait_ge(squares_summed, a)
                    nc.scalar.activation(squares[:], rows[:], ACT.Square).then_inc(squares_ready, 1)

                def copy_probs(item_c, p, j):
                    act.wait_ge(probs_turned, item_c * heads + j + 1)
                    nc.scalar.activation(probs_t[buffer(p, j)][:], turned_p[buffer(p, j)][:, 0:len(blocks) * P], ACT.Copy)\
                        .then_inc(probs_t_ready, 1)

                def exps(item_b, p, j):
                    act.wait_ge(max_ready, item_b * heads + j + 1)
                    for t in range(2):
                        k0, k1 = keys[t]
                        last = nc.scalar.activation(probs[p % 2][j][:, t, k0:k1],
                                                    scores_p[buffer(p, j)][:, t * SEQ + k0:t * SEQ + k1], ACT.Exp,
                                                    bias=neg_max[:, j, t:t + 1], accum_out=sums[:, j, t:t + 1])
                    last.then_inc(exp_done, 1)

                def copy_heads(item_c):
                    act.wait_ge(heads_done, item_c + 1)
                    nc.scalar.activation(heads_t[:], out_p[:, 0:SEQ], ACT.Copy).then_inc(heads_ready, 1)

                def start():
                    for a in range(2):
                        if rotary:
                            copy_rows(a)
                            square_rows(a)
                        elif not biased:
                            copy_qk(a, a)
                            copy_v(a, a)
                    if rotary:
                        for a in range(2):
                            copy_qk(a, a)
                            copy_v(a, a)
                        copy_rows(2)
                        square_rows(2)
                    for j in range(heads):
                        exps(0, 0, j)

                def item(quad, p, buffers, b, gp):
                    k = quad * 4 + p
                    if rotary:
                        copy_rows(k + 3)
                        for j in range(heads):
                            copy_probs(k, p, j)
                        square_rows(k + 3)
                    for j in range(heads):
                        exps(k + 1, p + 1, j)
                    copy_heads(k)
                    if not biased:
                        copy_qk(k + 2, p)
                        copy_v(k + 2, p, k + 1)

                schedule(act, start, item)

            @block.vector
            def _(dve):
                if window:
                    for p in range(2):
                        for j in range(heads):
                            nc.vector.memset(probs[p % 2][j][:, 1, 0:P - WINDOW], 0.0)

                def biased_qk(a, p, wb):
                    dve.wait_ge(qk_projected, a + 1)
                    nc.vector.tensor_scalar(qk[p % 2][:, 0:SEQ], qk_p[:, 0:SEQ], w[wb][:, 4 * P:4 * P + 1], scale, ALU.add,
                                            ALU.mult)
                    nc.vector.tensor_scalar(qk[p % 2][:, SEQ:], qk_p[:, SEQ:], w[wb][:, 4 * P + 1:4 * P + 2], None,
                                            ALU.add).then_inc(qk_ready, 1)

                def biased_v(a, p, wb):
                    dve.wait_ge(v_projected, a + 1)
                    bias = w[wb][:, 4 * P + 2:5 * P + 2].unsqueeze(1).to_broadcast([P, 2, P])
                    nc.vector.tensor_tensor(v[p % 2][:], v_p[:, 0:SEQ].rearrange("p (t d) -> p t d", t=2), bias, ALU.add)\
                        .then_inc(v_ready, 1)

                def sum_squares(a):
                    dve.wait_ge(squares_ready, a + 1)
                    if began(a):
                        dve.wait_ge(norms_ready, a)
                    nc.vector.tensor_reduce(square_sums[:], squares[:].rearrange("p t (h d) -> p (t h) d", d=hs), AX,
                                            ALU.add).then_inc(squares_summed, 1)
                    dve.wait_ge(squares_summed, a + 1)
                    nc.vector.tensor_scalar(square_sums[:], square_sums[:], 1e-24, None, ALU.max).then_inc(sums_ready, 1)

                def times_cos(a, p):
                    dve.wait_ge(rows_ready, a + 1)
                    if began(a - 1):
                        dve.wait_ge(rotated, a - 1)
                    nc.vector.tensor_tensor(by_cos[p % 2][:], rows[:], cos[:], ALU.mult)

                def times_sin(a):
                    if began(a):
                        dve.wait_ge(summed, a)
                    src, dst, table = (m[:].rearrange("p t (h s d) -> p (t h) s d", s=2, d=hs // 2)
                                       for m in (rows, by_sin, sin))
                    for s in range(2):
                        last = nc.vector.tensor_tensor(dst[:, :, s, :], src[:, :, 1 - s, :], table[:, :, s, :], ALU.mult)
                    last.then_inc(sin_done, 1)

                def maxima(item_b, p, j):
                    dve.wait_ge(scores_ready, item_b * heads + j + 1)
                    for t in range(2):
                        k0, k1 = keys[t]
                        last = nc.vector.tensor_reduce(neg_max[:, j, t:t + 1],
                                                       scores_p[buffer(p, j)][:, t * SEQ + k0:t * SEQ + k1], AX,
                                                       ALU.max, negate=True)
                    last.then_inc(max_ready, 1)

                def normalise_probs(item_b, p, j):
                    unit = item_b * heads + j
                    dve.wait_ge(exp_done, unit + 1)
                    nc.vector.reciprocal(inverse[:, j, :], sums[:, j, :]).then_inc(inverse_ready, 1)
                    dve.wait_ge(inverse_ready, unit + 1)
                    for t in range(2):
                        k0, k1 = keys[t]
                        last = nc.vector.tensor_scalar(probs[p % 2][j][:, t, k0:k1], probs[p % 2][j][:, t, k0:k1],
                                                       inverse[:, j, t:t + 1], None, ALU.mult)
                    last.then_inc(probs_ready, 1)

                def copy_probs(item_c, p, j):
                    dve.wait_ge(probs_turned, item_c * heads + j + 1)
                    nc.vector.tensor_copy(probs_t[buffer(p, j)][:], turned_p[buffer(p, j)][:, 0:len(blocks) * P])\
                        .then_inc(probs_t_ready, 1)

                def add_output(item_c, b):
                    dve.wait_ge(out_ready, item_c + 1)
                    mine = res[:, bass.ds(b * 2, 2), :]
                    nc.vector.tensor_tensor(mine, mine, out_p[:, SEQ:].rearrange("p (t d) -> p t d", t=2), ALU.add)\
                        .then_inc(added, 1)

                def start():
                    dve.sem_inc(added, 1)
                    for a in range(3 if rotary else 2):
                        if rotary:
                            times_cos(a, a)
                            sum_squares(a)
                            times_sin(a)
                        elif biased:
                            biased_qk(a, a, 0)
                            biased_v(a, a, 0)
                    for j in range(heads):
                        maxima(0, 0, j)
                        normalise_probs(0, 0, j)

                def item(quad, p, buffers, b, gp):
                    k = quad * 4 + p
                    if rotary:
                        times_cos(k + 3, p + 3)
                        for j in range(heads):
                            maxima(k + 1, p + 1, j)
                        sum_squares(k + 3)
                        normalise_probs(k + 1, p + 1, 0)
                        times_sin(k + 3)
                        normalise_probs(k + 1, p + 1, 1)
                        add_output(k, b)
                        return
                    for pass_ in range(0, heads, 2):
                        pass_heads = range(pass_, min(pass_ + 2, heads))
                        for j in pass_heads:
                            copy_probs(k, p, j)
                        for j in pass_heads:
                            maxima(k + 1, p + 1, j)
                        for j in pass_heads:
                            normalise_probs(k + 1, p + 1, j)
                    if biased:
                        biased_qk(k + 2, p, buffers[2])
                        dve.wait_ge(heads_done, k + 1)
                        biased_v(k + 2, p, buffers[2])
                    add_output(k, b)

                schedule(dve, start, item)


@as_stage
def feed_forward(core, name, w_dram, src_t, res, experts, parts, func, gated=False, biased=False, shares=None, layer=0):
    nc, E, C, H = core.nc, experts, CHUNKS, parts
    ups = H * P if gated else 0
    w2_at = (2 * H if gated else H) * P
    b1_at = w2_at + H * P
    b2_at = b1_at + (2 * H if gated else H)
    halves = min(E, 2)
    w_loads = (E // 2 + 1, max(E // 2, 1))
    in_flight = 2 if gated else 4

    w_loaded = core.sems(name, "w_loaded0", "w_loaded1")
    y_added = core.sems(name, "y_added0", "y_added1")
    hidden_psum, gate_ready, hidden_ready, y_ready = core.sems(name, "hidden_psum", "gate_ready", "hidden_ready", "y_ready")

    with ExitStack() as ctx:
        def sb(n, shape, dt=F32):
            return ctx.enter_context(nc.sbuf_tensor(f"{name}_{n}", shape, dt))

        w = [sb(f"w{i}", [P, w_dram.shape[2]]) for i in range(2)]
        hidden = [sb(f"hidden{i}", [P, H, CHUNK]) for i in range(2)]
        gate = [sb(f"gate{i}", [P, CHUNK]) for i in range(2)] if gated else None

        def unit_banks(p, h):
            u = (p * H + h) % in_flight
            return core.banks[2 * u:2 * u + 2] if gated else core.banks[u:u + 1]

        def gate_of(p, h):
            return gate[(p * H + h) % 2]

        y_p = core.banks[4:6]

        def schedule(eng, start, item, expert=None):
            start()

            def expert_pair(ep):
                for half in range(halves):
                    pair = ep * C + half * (C // 2)
                    e = ep * 2 + half
                    if expert:
                        expert(e, half, pair * 2)
                    with eng.Fori(0, C // 2 - 1) as i:
                        for p in range(2):
                            item(pair + i, p, half, half, i * 2 + p, i * 2 + p + 1, e, ep)
                    for p in range(2):
                        item(pair + C // 2 - 1, p, half, half if p == 0 else 1 - half, C - 2 + p, (C - 1 + p) % C, e, ep)

            if E > 2:
                with eng.Fori(0, E // 2) as ep:
                    expert_pair(ep)
            else:
                expert_pair(0)

        with nc.Block() as block:
            @block.sync
            def _(sp):
                def load_w(e, buffer):
                    src = w_dram[bass.ds(layer * E + e, 1), :, :].rearrange("a p n -> p (a n)")
                    sp.dma_start(w[buffer][:], src).then_inc(w_loaded[buffer], DMA)

                def start():
                    load_w(0, 0)

                def expert(e, half, first):
                    sp.wait_ge(y_ready, first + 1)
                    load_w(e + 1, 1 - half)

                schedule(sp, start, lambda *a: None, expert)
                for buffer in range(2):
                    sp.wait_ge(w_loaded[buffer], w_loads[buffer] * DMA)

            @block.tensor
            def _(pe):
                def hide(item_h, p, wb, c, first=False):
                    for h in range(H):
                        if not (first and h < in_flight) and h + 1 + H > in_flight:
                            pe.wait_ge(hidden_ready, item_h * H + h + 1 - in_flight)
                        for n, bank in enumerate(unit_banks(p, h)):
                            at = n * ups + h * P
                            last = nc.tensor.matmul(bank[:], w[wb][:, at:at + P], src_t[:, bass.ds(c * CHUNK, CHUNK)],
                                                    start=True, stop=True)
                        last.then_inc(hidden_psum, 1)

                def give(item_h, pair, p, wb):
                    pe.wait_ge(hidden_ready, (item_h + 1) * H)
                    pe.wait_ge(y_added[p], pair + 1)
                    for t in range(CHUNK // P):
                        for h in range(H):
                            last = nc.tensor.matmul(y_p[p][:, tile_of(t)], hidden[p][:, h, tile_of(t)],
                                                    w[wb][:, w2_at + h * P:w2_at + (h + 1) * P], start=h == 0,
                                                    stop=h == H - 1 and not biased)
                        if biased:
                            last = nc.tensor.matmul(y_p[p][:, tile_of(t)], core.ones[0:1, :], w[wb][0:1, b2_at:b2_at + P],
                                                    start=False, stop=True)
                    last.then_inc(y_ready, 1)

                def start():
                    pe.wait_ge(w_loaded[0], DMA)
                    hide(0, 0, 0, 0, first=True)

                def item(pair, p, now, nxt, c, c_next, e, ep):
                    k = pair * 2 + p
                    if now != nxt:
                        loads = ep + 1 if nxt else ep + 2
                        pe.wait_ge(w_loaded[nxt], loads * DMA)
                    hide(k + 1, 1 - p, nxt, c_next)
                    give(k, pair, p, now)

                schedule(pe, start, item)

            @block.scalar
            def _(act):
                def activate(item_h, p, wb):
                    for h in range(H):
                        act.wait_ge(hidden_psum, item_h * H + h + 1)
                        bias = {"bias": w[wb][:, b1_at + h:b1_at + h + 1]} if biased else {}
                        dst = gate_of(p, h)[:] if gated else hidden[p][:, h, :]
                        nc.scalar.activation(dst, unit_banks(p, h)[0][:], func, **bias)\
                            .then_inc(gate_ready if gated else hidden_ready, 1)

                def start():
                    activate(0, 0, 0)

                def item(pair, p, now, nxt, c, c_next, e, ep):
                    activate(pair * 2 + p + 1, 1 - p, nxt)

                schedule(act, start, item)

            @block.vector
            def _(dve):
                def times_gate(item_h, p, wb):
                    for h in range(H):
                        dve.wait_ge(gate_ready, item_h * H + h + 1)
                        up, dst = unit_banks(p, h)[1][:], hidden[p][:, h, :]
                        if biased:
                            bias = w[wb][:, b1_at + H + h:b1_at + H + h + 1]
                            last = nc.vector.scalar_tensor_tensor(dst, up, bias, gate_of(p, h)[:], ALU.add, ALU.mult)
                        else:
                            last = nc.vector.tensor_tensor(dst, up, gate_of(p, h)[:], ALU.mult)
                        last.then_inc(hidden_ready, 1)

                def start():
                    for p in range(2):
                        dve.sem_inc(y_added[p], 1)
                    if gated:
                        times_gate(0, 0, 0)

                def item(pair, p, now, nxt, c, c_next, e, ep):
                    k = pair * 2 + p
                    if gated:
                        times_gate(k + 1, 1 - p, nxt)
                    dve.wait_ge(y_ready, k + 1)
                    tiles = CHUNK // P
                    if shares is None:
                        mine = res[:, bass.ds(c * tiles, tiles), :]
                        last = nc.vector.tensor_tensor(mine, mine, y_p[p][:].rearrange("p (t d) -> p t d", t=tiles), ALU.add)
                    else:
                        for t in range(tiles):
                            mine = res[:, bass.ds(c * tiles + t, 1), :].rearrange("p a d -> p (a d)")
                            share = shares[:, bass.ds(e * TILES + c * tiles + t, 1)]
                            last = nc.vector.scalar_tensor_tensor(mine, y_p[p][:, tile_of(t)], share, mine, ALU.mult, ALU.add)
                    last.then_inc(y_added[p], 1)

                schedule(dve, start, item)


def router_logits(core, pe, src_t, wr, n, bank, done):
    for t in range(TILES):
        last = core.nc.tensor.matmul(bank[:, t * n:(t + 1) * n], src_t[:, tile_of(t)], wr[:, 0:n], start=True, stop=True)
    last.then_inc(done, 1)


def by_expert(tensor, n):
    return tensor[:, 0:TILES * n].rearrange("p (t e) -> p t e", e=n)


def first_best(nc, link, values, is_best, best, scratch, at_best, earliest, n):
    link(nc.vector.tensor_reduce(best[:], by_expert(values, n), AX, ALU.max))
    link(nc.vector.tensor_tensor(by_expert(scratch, n), by_expert(values, n), along(best[:], n), ALU.is_equal))
    link(nc.vector.tensor_tensor(scratch[:], scratch[:], earliest[:], ALU.mult))
    link(nc.vector.tensor_reduce(at_best[:], by_expert(scratch, n), AX, ALU.max))
    link(nc.vector.tensor_tensor(by_expert(is_best, n), by_expert(scratch, n), along(at_best[:], n), ALU.is_equal))


@as_stage
def route_top2(core, name, src_t, wr, shares, capacity=None, chunk=None):
    nc, n = core.nc, 8
    cols = TILES * n
    logits_ready, exp_in, exp_done, chosen_ready, counted, chained = core.sems(
        name, "logits_ready", "exp_in", "exp_done", "chosen_ready", "counted", "chained")
    with ExitStack() as ctx:
        def sb(nm, width):
            return ctx.enter_context(nc.sbuf_tensor(f"{name}_{nm}", [P, width], F32))

        value, first, second, scratch, weight, chosen, rank, spare = (
            sb(nm, cols) for nm in ("value", "first", "second", "scratch", "weight", "chosen", "rank", "spare"))
        best, best2, at_best, total, low = (sb(nm, TILES) for nm in ("best", "best2", "at_best", "total", "low"))
        offsets = [sb(f"offsets{i}", n) for i in range(2)]
        logits_p, before_p, tile_p = core.banks[0][:, 0:cols], core.banks[1], core.banks[2]

        with nc.Block() as block:
            @block.tensor
            def _(pe):
                router_logits(core, pe, src_t, wr, n, core.banks[0], logits_ready)
                pe.wait_ge(chosen_ready, 1)
                last = nc.tensor.matmul(before_p[:, 0:cols], core.is_before[:], chosen[:], start=True, stop=capacity is None)
                if capacity is not None:
                    halves = before_p[:, 0:cols].rearrange("p (b t e) -> p b t e", t=2, e=n)
                    firsts = chosen[:].rearrange("p (b t e) -> p b t e", t=2, e=n)
                    last = nc.tensor.matmul(halves[:, :, 1, :], core.ones[:], firsts[:, :, 0, :], start=False, stop=True)
                else:
                    last = nc.tensor.matmul(tile_p[:, 0:cols], core.ones[:], chosen[:], start=True, stop=True)
                last.then_inc(counted, 1)

            @block.scalar
            def _(act):
                act.wait_ge(exp_in, 1)
                if capacity is not None:
                    nc.scalar.activation(value[:], value[:], ACT.Exp).then_inc(exp_done, 1)
                else:
                    nc.scalar.activation(low[:], low[:], ACT.Exp).then_inc(exp_done, 1)

            @block.vector
            def _(dve):
                link = chain(dve, chained)
                v = nc.vector

                def add_weighted(out, choice, w):
                    link(v.tensor_tensor(by_expert(out, n), by_expert(choice, n), along(w[:], n), ALU.mult))

                dve.wait_ge(logits_ready, 1)
                link(v.tensor_copy(value[:], logits_p))
                if capacity is not None:
                    link(v.tensor_reduce(best[:], by_expert(value, n), AX, ALU.max))
                    v.tensor_tensor(by_expert(value, n), by_expert(value, n), along(best[:], n), ALU.subtract)\
                        .then_inc(exp_in, 1)
                    dve.wait_ge(exp_done, 1)
                    link(v.tensor_reduce(total[:], by_expert(value, n), AX, ALU.add))
                    link(v.reciprocal(total[:], total[:]))
                    link(v.tensor_tensor(by_expert(value, n), by_expert(value, n), along(total[:], n), ALU.mult))
                first_best(nc, link, value, first, best, scratch, at_best, core.earliest, n)
                link(v.scalar_tensor_tensor(spare[:], first[:], NEG, value[:], ALU.mult, ALU.add))
                first_best(nc, link, spare, second, best2, scratch, at_best, core.earliest, n)
                v.tensor_tensor(chosen[:], first[:], second[:], ALU.add).then_inc(chosen_ready, 1)
                out = shares[:, 0:cols].rearrange("p (e t) -> p t e", t=TILES)
                if capacity is not None:
                    dve.wait_ge(counted, 1)
                    link(v.scalar_tensor_tensor(weight[:], before_p[:, 0:cols], float(capacity), chosen[:], ALU.is_lt,
                                                ALU.mult))
                    link(v.tensor_tensor(out, by_expert(weight, n), by_expert(value, n), ALU.mult))
                    return
                v.tensor_tensor(low[:], best2[:], best[:], ALU.subtract).then_inc(exp_in, 1)
                dve.wait_ge(exp_done, 1)
                link(v.tensor_scalar(total[:], low[:], 1.0, None, ALU.add))
                link(v.reciprocal(total[:], total[:]))
                link(v.tensor_tensor(low[:], low[:], total[:], ALU.mult))
                add_weighted(weight, first, total)
                add_weighted(scratch, second, low)
                link(v.tensor_tensor(weight[:], weight[:], scratch[:], ALU.add))
                dve.wait_ge(counted, 1)
                link(v.tensor_copy(spare[:], tile_p[:, 0:cols]))
                have, other, step = spare, scratch, n
                while step < cols:
                    link(v.tensor_copy(other[:, 0:step], have[:, 0:step]))
                    link(v.tensor_tensor(other[:, step:], have[:, step:], have[:, 0:cols - step], ALU.add))
                    have, other, step = other, have, 2 * step
                link(v.tensor_tensor(rank[:], have[:], tile_p[:, 0:cols], ALU.subtract))
                link(v.tensor_tensor(rank[:], rank[:], before_p[:, 0:cols], ALU.add))
                link(v.memset(offsets[0][:], 0.0))
                link(v.tensor_copy(offsets[0][:, 1:n], have[:, cols - n:cols - 1]))
                step = 1
                have, other = offsets
                while step < n:
                    link(v.tensor_copy(other[:, 0:step], have[:, 0:step]))
                    link(v.tensor_tensor(other[:, step:], have[:, step:], have[:, 0:n - step], ALU.add))
                    have, other, step = other, have, 2 * step
                link(v.tensor_tensor(by_expert(rank, n), by_expert(rank, n),
                                     have[:].unsqueeze(1).to_broadcast([P, TILES, n]), ALU.add))
                link(v.tensor_scalar(spare[:], rank[:], float(chunk), None, ALU.is_ge))
                for c in range(2, n):
                    link(v.scalar_tensor_tensor(spare[:], rank[:], float(c * chunk), spare[:], ALU.is_ge, ALU.add))
                for c in range(n):
                    link(v.scalar_tensor_tensor(scratch[:], spare[:], float(c), weight[:], ALU.is_equal, ALU.mult))
                    link(v.tensor_reduce(shares[:, c * TILES:(c + 1) * TILES], by_expert(scratch, n), AX, ALU.add))


@as_stage
def route_top8(core, name, src_t, wr, bias, shares, route_scale):
    nc, n = core.nc, 16
    cols = TILES * n
    logits_ready, scores_ready, chained = core.sems(name, "logits_ready", "scores_ready", "chained")
    with ExitStack() as ctx:
        def sb(nm, width):
            return ctx.enter_context(nc.sbuf_tensor(f"{name}_{nm}", [P, width], F32))

        score, select, left, top = sb("score", cols), sb("select", cols), sb("left", cols), sb("top", TILES * 8)
        total = sb("total", TILES)
        with nc.Block() as block:
            @block.tensor
            def _(pe):
                router_logits(core, pe, src_t, wr, n, core.banks[0], logits_ready)

            @block.scalar
            def _(act):
                act.wait_ge(logits_ready, 1)
                nc.scalar.activation(score[:], core.banks[0][:, 0:cols], ACT.Sigmoid).then_inc(scores_ready, 1)

            @block.vector
            def _(dve):
                link = chain(dve, chained)
                v = nc.vector
                dve.wait_ge(scores_ready, 1)
                link(v.tensor_tensor(by_expert(select, n), by_expert(score, n), bias.unsqueeze(1).to_broadcast([P, TILES, n]),
                                     ALU.add))
                for t in range(TILES):
                    link(v.max(top[:, t * 8:(t + 1) * 8], select[:, t * n:(t + 1) * n]))
                    link(v.match_replace(left[:, t * n:(t + 1) * n], top[:, t * 8:(t + 1) * 8],
                                         select[:, t * n:(t + 1) * n], NEG))
                link(v.scalar_tensor_tensor(left[:], left[:], NEG, score[:], ALU.is_equal, ALU.mult))
                link(v.tensor_reduce(total[:], by_expert(left, n), AX, ALU.add))
                link(v.reciprocal(total[:], total[:]))
                link(v.tensor_scalar(total[:], total[:], route_scale, None, ALU.mult))
                out = shares[:, 0:cols].rearrange("p (e t) -> p t e", t=TILES)
                link(v.tensor_tensor(out, by_expert(left, n), along(total[:], n), ALU.mult))


@as_stage
def load_rotary(core, base, src):
    (loaded,) = core.sems("rotary", "loaded")
    with core.nc.Block() as block:
        @block.sync
        def _(sp):
            sp.dma_start(base[:], src).then_inc(loaded, DMA)
            sp.wait_ge(loaded, DMA)


@as_stage
def rotary_tables(core, name, cos, sin, base, scales_dram, layer):
    nc = core.nc
    (loaded,) = core.sems(name, "loaded")
    with ExitStack() as ctx:
        scales = ctx.enter_context(nc.sbuf_tensor(f"{name}_scales", [P, 2, 2 * P], F32))
        with nc.Block() as block:
            @block.sync
            def _(sp):
                src = scales_dram[bass.ds(layer, 1), :].rearrange("a n -> (a n)").partition_broadcast(P)
                sp.dma_start(scales[:].rearrange("p a n -> p (a n)"), src).then_inc(loaded, DMA)

            @block.vector
            def _(dve):
                dve.wait_ge(loaded, DMA)
                for n, table in enumerate((cos, sin)):
                    nc.vector.tensor_tensor(table[:], base[:, n], scales[:, n, :].unsqueeze(1).to_broadcast([P, 2, 2 * P]),
                                            ALU.mult)


def build(nc, t, out, upto=99):
    with ExitStack() as ctx:
        core = Core(nc, ctx)
        res = core.keep("residual", [P, TILES, D])
        xn_t = core.keep("normed_t", [P, TOKENS])
        core.ident, core.is_before, core.ones = (core.keep(n, [P, P]) for n in ("ident", "is_before", "ones"))
        core.ident_bf = core.keep("ident_bf", [P, P], BF16)
        core.minus_half = core.keep("minus_half", [P, TILES])
        core.earliest = core.keep("earliest", [P, TILES * 8])
        masks = core.keep("masks_f32", [P, 3 * P + WINDOW])
        core.masks = core.keep("masks", [P, 3 * P + WINDOW], BF16)
        core.causal_mask, core.window_mask = core.masks[:, 0:P], core.masks[:, P:3 * P + WINDOW]
        shares = core.keep("shares", [P, TILES * 16])
        wr0, wr1, wr3 = core.keep("wr0", [P, 8]), core.keep("wr1", [P, 16]), core.keep("wr3", [P, 8])
        bo0, bo3, bias1 = core.keep("bo0", [P, D]), core.keep("bo3", [P, D]), core.keep("bias1", [P, 16])

        def rows(name):
            return t[name].partition_broadcast(P)

        load(core, [(res[:], t["x"].rearrange("b (t p) d -> p (b t) d", p=P)), (core.ident[:], t["ident"]),
                    (core.is_before[:], t["is_before"]), (core.earliest[:], rows("earliest")), (masks[:], t["masks"]),
                    (wr0[:], t["wr0"]), (wr1[:], t["wr1"]), (wr3[:], t["wr3"]), (bo0[:], rows("bo0")),
                    (bo3[:], rows("bo3")), (bias1[:], rows("bias1"))], masks)

        if 0 < upto < 20 or upto > 30:
            normalise(core, "n0", res, xn_t)
            route_top2(core, "r0", xn_t, wr0, shares, capacity=int(SEQ / 8 * 1.25))
            if upto != 11:
                add_row(core, "b0", res, bo0[:])
                attention(core, "a0", t["a0"], xn_t, res, groups=8, heads=2, scale=64 ** -0.5)
            if upto != 10:
                feed_forward(core, "f0", t["f0"], xn_t, res, 8, 4, ACT.Relu, biased=True, shares=shares)
        if 1 < upto < 10 or upto > 30:
            normalise(core, "n1", res, xn_t)
            route_top8(core, "r1", xn_t, wr1, bias1[:], shares, 2.826)
            attention(core, "a1", t["a1"], xn_t, res, groups=8, heads=2, causal=True, scale=64 ** -0.5)
            feed_forward(core, "f1", t["f1"], xn_t, res, 16, 1, ACT.Silu, gated=True, shares=shares)
            feed_forward(core, "f1s", t["f1s"], xn_t, res, 1, 1, ACT.Silu, gated=True)
        if 2 < upto < 10 or upto > 30 or upto == 20:
            with ExitStack() as inner:
                y = inner.enter_context(nc.sbuf_tensor("inner", [P, TILES, D], F32))
                y_t = inner.enter_context(nc.sbuf_tensor("inner_t", [P, TOKENS], F32))
                base = inner.enter_context(nc.sbuf_tensor("rotary", [P, 2, 2, 2 * P], F32))
                cos, sin = (inner.enter_context(nc.sbuf_tensor(n, [P, 2, 2 * P], F32)) for n in ("cos", "sin"))
                normalise(core, "n2", res, xn_t, rows=y)
                load_rotary(core, base, t["rotary"])
                attention(core, "a2", t["a2"], xn_t, res, groups=1, heads=1, causal=True, scale=float(D) ** -0.5,
                          biased=True)
                with nc.Fori(0, DEPTH) as layer:
                    rotary_tables(core, "t2", cos, sin, base, t["qk_scales"], layer)
                    normalise(core, "s2", y, y_t, shift=True, norm=False, layer=layer)
                    attention(core, "w2", t["w2"], y_t, y, groups=8, heads=2, window=True, rotary=(cos, sin), layer=layer)
                    normalise(core, "m2", y, y_t, shift=True, gain_bias=t["gain_bias"], layer=layer)
                    feed_forward(core, "f2", t["f2"], y_t, y, 1, 3, ACT.Gelu, gated=True, biased=True, layer=layer)
                add_rows(core, res, y)
        if 3 < upto < 10 or upto > 30 or upto == 21:
            normalise(core, "n3", res, xn_t)
            route_top2(core, "r3", xn_t, wr3, shares, chunk=TOKENS * 2 // 8)
            add_row(core, "b3", res, bo3[:])
            attention(core, "a3", t["a3"], xn_t, res, groups=4, heads=4, scale=8 ** -0.5, biased=True)
            feed_forward(core, "f3", t["f3"], xn_t, res, 8, 4, ACT.Gelu, shares=shares)
        store(core, res, out)


def constants():
    i = np.arange(P)
    late = np.arange(P + WINDOW)
    masks = [np.where(i[None, :] <= i[:, None], 0.0, NEG),
             np.where((i[None, :] <= i[:, None]) & (i[None, :] >= i[:, None] - WINDOW), 0.0, NEG),
             np.where((late[None, :] >= i[:, None]) & (late[None, :] <= i[:, None] + WINDOW), 0.0, NEG)]
    half = np.arange(0, 64, 2, dtype=np.float32)
    freqs = np.arange(SEQ, dtype=np.float32)[:, None] * (1.0 / 10000.0 ** (half / np.float32(64)))[None, :]
    freqs = np.concatenate([freqs, freqs], -1).astype(np.float32)
    power = (np.arange(SEQ, dtype=np.float32) - SEQ // 2) / (WINDOW // 2)
    scale = ((half + 0.4 * 64) / (1.4 * 64))[None, :].astype(np.float32) ** power[:, None]
    scale = np.concatenate([scale, scale], -1).astype(np.float32)
    sign = np.where(np.arange(64) < 32, -1.0, 1.0)
    tables = np.empty((2, SEQ, 2, 2, 64), np.float32)
    for n, turn in enumerate((np.cos(freqs), np.sin(freqs) * sign)):
        tables[n, :, 0] = (8.0 * turn * scale)[:, None]
        tables[n, :, 1] = (turn / scale)[:, None]
    rotary = tables.reshape(2, 2, P, 2 * P).transpose(2, 0, 1, 3)
    return {
        "ident": np.eye(P), "is_before": i[:, None] < i[None, :], "masks": np.concatenate(masks, 1),
        "earliest": np.tile(8 - np.arange(8), TILES), "rotary": rotary,
    }


def beside(*parts):
    return np.concatenate(parts, axis=-1)


def first_row(row):
    block = np.zeros((P, row.shape[-1]), np.float32)
    block[0] = row
    return block


def in_parts(w2):
    return w2.reshape(-1, P, w2.shape[-1]).transpose(1, 0, 2).reshape(P, -1)


def padded(groups):
    return np.stack(groups + [np.zeros_like(groups[0])])


def lay_out(i):
    def heads_of_two(q, k, v, o):
        return [beside(q[:, s], k[:, s], v[:, s], o[s, :]) for s in (slice(g * P, (g + 1) * P) for g in range(8))]

    def spread(m):
        wide = np.zeros(m.shape[:-1] + (4, 4, 32), np.float32)
        wide[..., :8] = m.reshape(m.shape[:-1] + (4, 4, 8))
        return [wide[..., g, :, :].reshape(m.shape[:-1] + (P,)) for g in range(4)]

    def column(row):
        return row[:, None]

    def on_all(row):
        return np.broadcast_to(row, (P, row.shape[-1]))

    inner, t = 1024, constants()
    t["x"] = i["L0_attn_hidden_states"]
    wkv = i["L0_attn_Wkv"]
    t["a0"] = padded(heads_of_two(i["L0_attn_Wq"], wkv[:, :inner], wkv[:, inner:], i["L0_attn_Wo"]))
    t["bo0"], t["wr0"] = i["L0_attn_bo"], i["L0_ffn_Wr"]
    t["f0"] = padded([beside(i["L0_ffn_W1"][e], in_parts(i["L0_ffn_W2"][e]), i["L0_ffn_b1"][e].reshape(4, P).T,
                             first_row(i["L0_ffn_b2"][e])) for e in range(8)])
    w = i["L1_attn_W_qkv"]
    t["a1"] = padded(heads_of_two(w[:, :inner], w[:, inner:2 * inner], w[:, 2 * inner:], i["L1_attn_W_out"]))
    t["wr1"], t["bias1"] = i["L1_ffn_gate_w"].T, i["L1_ffn_expert_bias"]
    t["f1"] = padded([beside(i["L1_ffn_w_gate"][e].T, i["L1_ffn_w_up"][e].T, i["L1_ffn_w_down"][e].T) for e in range(16)])
    t["f1s"] = padded([beside(i["L1_ffn_shared_gate_w"].T, i["L1_ffn_shared_up_w"].T, i["L1_ffn_shared_down_w"].T)])
    t["a2"] = padded([beside(i["L2_attn_Wq"].T, i["L2_attn_Wk"].T, i["L2_attn_Wv"].T, np.eye(P, dtype=np.float32),
                             column(i["L2_attn_bq"]), column(i["L2_attn_bk"]), on_all(i["L2_attn_bv"]))])
    groups = []
    for n in range(DEPTH):
        w = i["L2_ffn_Wqkv"][n]
        groups += heads_of_two(w[:, :inner], w[:, inner:2 * inner], w[:, 2 * inner:], i["L2_ffn_Wo"][n])
    t["w2"] = padded(groups)
    qs, ks = i["L2_ffn_q_scale"], i["L2_ffn_k_scale"]
    turned = [np.concatenate([s[:, 32:], s[:, :32]], 1) for s in (qs, ks)]
    t["qk_scales"] = beside(qs, qs, ks, ks, turned[0], turned[0], turned[1], turned[1])
    t["gain_bias"] = np.stack([i["L2_ffn_ln_g"], i["L2_ffn_ln_b"]], -1)
    layers = []
    for n in range(DEPTH):
        w1 = np.zeros((2, P, 3 * P), np.float32)
        b1 = np.zeros((2, 3 * P), np.float32)
        hidden = i["L2_ffn_W2"].shape[1]
        for half, at in enumerate((hidden, 0)):
            w1[half, :, :hidden] = i["L2_ffn_W1"][n][:, at:at + hidden]
            b1[half, :hidden] = i["L2_ffn_b1"][n][at:at + hidden]
        w2 = np.zeros((3 * P, P), np.float32)
        w2[:hidden] = i["L2_ffn_W2"][n]
        layers.append(beside(w1[0], w1[1], in_parts(w2), b1[0].reshape(3, P).T, b1[1].reshape(3, P).T,
                             first_row(i["L2_ffn_b2"][n])))
    t["f2"] = padded(layers)
    q, k, v = (spread(i[f"L3_attn_W{c}"]) for c in "qkv")
    bq, bk, bv = (spread(i[f"L3_attn_b{c}"]) for c in "qkv")
    wo = [m.T for m in spread(i["L3_attn_Wo"].T)]
    t["a3"] = padded([beside(q[g], k[g], v[g], wo[g], column(bq[g]), column(bk[g]), on_all(bv[g])) for g in range(4)])
    t["bo3"], t["wr3"] = i["L3_attn_bo"], i["L3_ffn_Wr"].T
    t["f3"] = padded([beside(i["L3_ffn_W1"][e], in_parts(i["L3_ffn_W2"][e])) for e in range(8)])
    return {name: np.ascontiguousarray(a, dtype=np.float32) for name, a in t.items()}


def kernel(**inputs):
    from concourse import bacc
    from concourse.bass_utils import run_bass_kernel_spmd

    arrays = lay_out({name: np.asarray(a) for name, a in inputs.items()})
    nc = bacc.Bacc("TRN2", target_bir_lowering=False, num_devices=1)
    tensors = {name: nc.dram_tensor(f"in_{name}", a.shape, F32, kind="ExternalInput").ap() for name, a in arrays.items()}
    out = nc.dram_tensor("out", (BATCH, SEQ, D), F32, kind="ExternalOutput").ap()
    build(nc, tensors, out)
    results = run_bass_kernel_spmd(nc, [{f"in_{name}": a for name, a in arrays.items()}], core_ids=[0])
    return results.results[0]["out"]
```

```python
from contextlib import ExitStack, contextmanager

import numpy as np

import concourse.bass as bass
from concourse import mybir

F32 = mybir.dt.float32
ALU = mybir.AluOpType
ACT = mybir.ActivationFunctionType
AX = mybir.AxisListType.X

P = 128
BATCH, SEQ, D = 16, 256, 128
TOKENS = BATCH * SEQ
TILES = TOKENS // P
DEPTH = 6
WINDOW = 32
EPS = 1e-5
NEG = -1e30
BANK = 512
EXPERTS = 8
CAPACITY = int(SEQ / EXPERTS * 1.25)
CHUNK = 512
CHUNKS = TOKENS // CHUNK
DMA = 16


class Core:

    def __init__(self, nc, ctx):
        self.nc, self.ctx = nc, ctx
        self.banks = [ctx.enter_context(nc.psum_tensor(f"bank{i}", [P, BANK], F32)) for i in range(8)]

    def keep(self, name, shape, dt=F32):
        return self.ctx.enter_context(self.nc.sbuf_tensor(name, shape, dt))

    def sems(self, stage, *names):
        return [self.nc.alloc_semaphore(f"{stage}_{n}") for n in names]


@contextmanager
def stage(core):
    before = core.nc.snapshot_sems()
    yield
    core.nc.clear_and_free_semaphores(core.nc.allocated_since(before))
    core.nc.all_engine_barrier()


def as_stage(build_stage):
    def wrapped(core, *args, **kwargs):
        with stage(core):
            build_stage(core, *args, **kwargs)

    return wrapped


def chain(eng, sem, base=0):
    done = [0]

    def link(ins):
        done[0] += 1
        ins.then_inc(sem, 1)
        eng.wait_ge(sem, base + done[0])

    return link


def began(count):
    return not isinstance(count, int) or count > 0


def tile_of(n):
    return slice(n * P, (n + 1) * P)


def along(column, n):
    return column.unsqueeze(2).to_broadcast([column.shape[0], column.shape[1], n])


def buffer_of(heads):
    return lambda p, j: (p * heads + j) % 2


@as_stage
def load(core, pairs):
    nc = core.nc
    (loaded,) = core.sems("load", "loaded")
    with nc.Block() as block:
        @block.sync
        def _(sp):
            for dst, src in pairs:
                sp.dma_start(dst, src).then_inc(loaded, DMA)

        @block.vector
        def _(dve):
            dve.wait_ge(loaded, DMA * len(pairs))
            nc.vector.memset(core.minus_half[:], -0.5)
            nc.vector.memset(core.ones[:], 1.0)


def add_row(core, name, res, row):
    nc = core.nc
    with nc.Block() as block:
        @block.vector
        def _(dve):
            nc.vector.tensor_tensor(res[:], res[:], row.unsqueeze(1).to_broadcast([P, TILES, D]), ALU.add)


def add_rows(core, res, more):
    nc = core.nc
    with nc.Block() as block:
        @block.vector
        def _(dve):
            nc.vector.tensor_tensor(res[:], res[:], more[:], ALU.add)


@as_stage
def store(core, res, out):
    nc = core.nc
    (stored,) = core.sems("store", "stored")
    with nc.Block() as block:
        @block.sync
        def _(sp):
            sp.dma_start(out.rearrange("b (t p) d -> p (b t) d", p=P), res[:]).then_inc(stored, DMA)
            sp.wait_ge(stored, DMA)


@as_stage
def transpose_shifted(core, name, src, dst_t):
    nc, H, N = core.nc, D // 2, TOKENS // BANK
    (in_psum,) = core.sems(name, "in_psum")
    by_batch = dst_t[:].rearrange("p (b s) -> p b s", s=SEQ)
    batches = BANK // SEQ

    def move(q, copy):
        copy(dst_t[0:H, q * BANK:(q + 1) * BANK], core.banks[q][0:H, :])
        copy(by_batch[H:P, q * batches:(q + 1) * batches, 1:SEQ],
             core.banks[q][H:P, :].rearrange("p (b s) -> p b s", s=SEQ)[:, :, 0:SEQ - 1])

    with nc.Block() as block:
        @block.tensor
        def _(pe):
            for q in range(N):
                for i in range(BANK // P):
                    last = nc.tensor.transpose(core.banks[q][:, tile_of(i)], src[:, BANK // P * q + i, :], core.ident[:])
                last.then_inc(in_psum, 1)

        @block.scalar
        def _(act):
            for q in range(0, N, 2):
                act.wait_ge(in_psum, q + 1)
                move(q, lambda dst, src: nc.scalar.activation(dst, src, ACT.Copy))

        @block.vector
        def _(dve):
            nc.vector.memset(by_batch[H:P, :, 0:1], 0.0)
            for q in range(1, N, 2):
                dve.wait_ge(in_psum, q + 1)
                move(q, nc.vector.tensor_copy)


@as_stage
def normalise(core, name, src, dst_t, rows=None, gain_bias=None, layer=0):
    nc, H, shift = core.nc, D // 2, gain_bias is not None
    size = 8
    chunks, per_bank = TILES // size, BANK // P
    shifted = core.sems(name, *(f"shifted{c}" for c in range(chunks)))
    zeroed, copied, summed, mean_ready, squared, var_ready, rstd_ready, rows_ready, in_psum, gains_loaded = core.sems(
        name, "zeroed", "copied", "summed", "mean_ready", "squared", "var_ready", "rstd_ready", "rows_ready", "in_psum",
        "gains_loaded")

    def of_chunk(c):
        return slice(c * size, (c + 1) * size)

    with ExitStack() as ctx:
        def sb(n, shape, dt=F32):
            return ctx.enter_context(nc.sbuf_tensor(f"{name}_{n}", shape, dt))

        work = sb("work", [P, TILES, D]) if shift else src
        normed = rows if rows is not None else sb("normed", [P, TILES, D])
        neg_mean, var, rstd = (sb(n, [P, TILES]) for n in ("neg_mean", "var", "rstd"))
        gains = sb("gains", [P, 2])

        with nc.Block() as block:
            if shift:
                @block.sync
                def _(sp):
                    src_gb = gain_bias[bass.ds(layer, 1), :, :].rearrange("a p n -> p (a n)")
                    sp.dma_start(gains[:], src_gb).then_inc(gains_loaded, DMA)
                    sp.wait_ge(zeroed, 1)
                    for c in range(chunks):
                        sp.dma_start(work[1:P, of_chunk(c), H:D], src[0:P - 1, of_chunk(c), H:D]).then_inc(shifted[c], DMA)
                        into = work[0:1, of_chunk(c), H:D].rearrange("p (b t) d -> p b t d", t=2)
                        last = src[P - 1:P, of_chunk(c), H:D].rearrange("p (b t) d -> p b t d", t=2)
                        sp.dma_start(into[:, :, 1, :], last[:, :, 0, :]).then_inc(shifted[c], DMA)

            @block.vector
            def _(dve):
                def sums(c):
                    if shift:
                        dve.wait_ge(copied, c + 1)
                        dve.wait_ge(shifted[c], 2 * DMA)
                    at = neg_mean[:, of_chunk(c)]
                    nc.vector.tensor_reduce(at, work[:, of_chunk(c), :], AX, ALU.add).then_inc(summed, 1)
                    dve.wait_ge(summed, c + 1)
                    nc.vector.tensor_scalar(at, at, -1.0 / D, None, ALU.mult).then_inc(mean_ready, 1)

                if shift:
                    nc.vector.memset(work[0:1, :, H:D], 0.0).then_inc(zeroed, 1)
                sums(0)
                sums(1)
                for c in range(chunks):
                    if c + 2 < chunks:
                        sums(c + 2)
                    dve.wait_ge(rstd_ready, c + 1)
                    for t in range(c * size, (c + 1) * size):
                        last = nc.vector.tensor_scalar(normed[:, t, :], work[:, t, :], neg_mean[:, t:t + 1], rstd[:, t:t + 1],
                                                       ALU.add, ALU.mult)
                        if t % per_bank == per_bank - 1:
                            last.then_inc(rows_ready, 1)

            @block.gpsimd
            def _(pool):
                if shift:
                    for c in range(chunks):
                        nc.gpsimd.tensor_copy(work[:, of_chunk(c), 0:H], src[:, of_chunk(c), 0:H]).then_inc(copied, 1)
                for c in range(chunks):
                    at = var[:, of_chunk(c)]
                    pool.wait_ge(squared, c + 1)
                    nc.gpsimd.tensor_scalar(at, at, 1.0 / D, EPS, ALU.mult, ALU.add).then_inc(var_ready, 1)
                    pool.wait_ge(var_ready, c + 1)
                    nc.gpsimd.tensor_tensor(rstd[:, of_chunk(c)], at, core.minus_half[:, 0:size], ALU.pow)\
                        .then_inc(rstd_ready, 1)

            @block.scalar
            def _(act):
                def square(c):
                    act.wait_ge(mean_ready, c + 1)
                    for t in range(c * size, (c + 1) * size):
                        last = nc.scalar.activation(normed[:, t, :], work[:, t, :], ACT.Square, bias=neg_mean[:, t:t + 1],
                                                    accum_out=var[:, t:t + 1])
                    last.then_inc(squared, 1)

                def move(c):
                    for q in range(c * size // per_bank, (c + 1) * size // per_bank):
                        act.wait_ge(in_psum, q + 1)
                        dst = dst_t[:, q * BANK:(q + 1) * BANK]
                        if shift:
                            nc.scalar.activation(dst, core.banks[q][:], ACT.Identity, scale=gains[:, 0:1],
                                                 bias=gains[:, 1:2])
                        else:
                            nc.scalar.activation(dst, core.banks[q][:], ACT.Copy)

                square(0)
                square(1)
                square(2)
                if shift:
                    act.wait_ge(gains_loaded, DMA)
                move(0)
                square(3)
                for c in range(1, chunks):
                    move(c)

            @block.tensor
            def _(pe):
                for q in range(TILES // per_bank):
                    pe.wait_ge(rows_ready, q + 1)
                    for i in range(per_bank):
                        last = nc.tensor.transpose(core.banks[q][:, tile_of(i)], normed[:, per_bank * q + i, :],
                                                   core.ident[:])
                    last.then_inc(in_psum, 1)


@as_stage
def attention(core, name, w_dram, src_t, res, groups, heads, causal=False, window=False, scale=None,
              biased=False, rotary=None, layer=0):
    nc, hs, G, NB = core.nc, P // heads, groups, BATCH
    masked = causal or window
    keys = [(0, P), (P - WINDOW, 2 * P)] if window else [(0, P), (0, 2 * P)] if causal else [(0, 2 * P)] * 2
    blocks = [(0, 0), (0, 1), (1, 1)] if masked else [(0, 0), (0, 1), (1, 0), (1, 1)]
    late = P if masked else 0
    halves = min(G, 2)
    w_loads = (G // 2 + 1, max(G // 2, 1))
    ahead = 3 if rotary else 2
    shared = max(64 // hs, 1)
    product_rows = max(hs, 64)
    copies_by_act = heads == 4 or bool(rotary)

    x_loaded = core.sems(name, *(f"x_loaded{i}" for i in range(4)))
    w_loaded = core.sems(name, "w_loaded0", "w_loaded1")
    (qk_projected, v_projected, qk_ready, v_ready, scores_ready, max_ready, exp_done, inverse_ready, probs_ready,
     probs_turned, probs_t_ready, heads_done, heads_ready, out_ready, added) = core.sems(
        name, "qk_projected", "v_projected", "qk_ready", "v_ready", "scores_ready", "max_ready", "exp_done",
        "inverse_ready", "probs_ready", "probs_turned", "probs_t_ready", "heads_done", "heads_ready", "out_ready",
        "added")
    if rotary:
        projected, rows_ready, squares_ready, sums_ready, norms_ready, sin_done, summed, rotated, squares_summed = core.sems(
            name, "projected", "rows_ready", "squares_ready", "sums_ready", "norms_ready", "sin_done", "summed",
            "rotated", "squares_summed")

    with ExitStack() as ctx:
        def sb(n, shape, dt=F32):
            return ctx.enter_context(nc.sbuf_tensor(f"{name}_{n}", shape, dt))

        w = [sb(f"w{i}", [P, w_dram.shape[2]]) for i in range(2)]
        x = [sb(f"x{i}", [P, SEQ]) for i in range(4)]
        qk = [sb(f"qk{i}", [P, (shared + 1) * SEQ]) for i in range(2)]
        keys_at = shared * SEQ
        v = [sb(f"v{i}", [P, 2, P]) for i in range(2)]
        probs = [[sb(f"probs{i}_{j}", [P, 2, SEQ]) for j in range(heads)] for i in range(2)]
        probs_t = [sb(f"probs_t{i}", [P, len(blocks) * P]) for i in range(2)]
        heads_t = sb("heads_t", [P, SEQ])
        waited = sb("waited", [P, heads])
        neg_max, sums, inverse = (sb(n, [P, heads, 2]) for n in ("neg_max", "sums", "inverse"))
        if rotary:
            cos, sin = rotary
            squares, by_sin, rot = (sb(n, [P, 2, 2 * P]) for n in ("squares", "by_sin", "rot"))
            rows, by_cos = ([sb(f"{n}{i}", [P, 2, 2 * P]) for i in range(2)] for n in ("rows", "by_cos"))
            square_sums, norms = sb("square_sums", [P, 8]), sb("norms", [P, 8])
            rows_p = core.banks[2]
        qk_p, v_p = core.banks[0], core.banks[1]
        out_p = core.banks[3]
        scores_p, turned_p = core.banks[4:6], core.banks[6:8]

        def schedule(eng, start, item, group=None):
            start()

            def group_pair(gp):
                for half in range(halves):
                    quad = gp * (NB // 2) + half * (NB // 4)
                    if group:
                        group(gp * 2 + half, half, quad * 4)
                    with eng.Fori(0, NB // 4 - 1) as i:
                        for p in range(4):
                            item(quad + i, p, [half] * 4, i * 4 + p, gp)
                    for p in range(4):
                        item(quad + NB // 4 - 1, p, [half if p + n < 4 else 1 - half for n in range(4)], NB - 4 + p, gp)

            if G > 2:
                with eng.Fori(0, G // 2) as gp:
                    group_pair(gp)
            else:
                group_pair(0)

        buffer = buffer_of(heads)

        with nc.Block() as block:
            @block.sync
            def _(sp):
                def load_x(p, b):
                    sp.dma_start(x[p][:], src_t[:, bass.ds(b * SEQ, SEQ)]).then_inc(x_loaded[p], DMA)

                def start():
                    for b in range(4):
                        load_x(b, b)

                def item(quad, p, buffers, b, gp):
                    sp.wait_ge(v_projected, quad * 4 + p + 1)
                    load_x(p, b + 4 if not isinstance(b, int) else (b + 4) % NB)

                schedule(sp, start, item)
                for p in range(4):
                    sp.wait_ge(x_loaded[p], (G * NB // 4 + 1) * DMA)

            @block.gpsimd
            def _(pool):
                def load_w(g, buffer):
                    src = w_dram[bass.ds(layer * G + g, 1), :, :].rearrange("a p n -> p (a n)")
                    pool.dma_start(w[buffer][:], src).then_inc(w_loaded[buffer], DMA)

                def norm_factors(a, p):
                    both = by_cos[p % 2]
                    pool.wait_ge(sums_ready, a + 1)
                    if began(a):
                        pool.wait_ge(rotated, a)
                    nc.gpsimd.tensor_tensor(norms[:], square_sums[:], core.minus_half[:, 0:8], ALU.pow)\
                        .then_inc(norms_ready, 1)
                    pool.wait_ge(sin_done, a + 1)
                    nc.gpsimd.tensor_tensor(both[:], both[:], by_sin[:], ALU.add).then_inc(summed, 1)
                    pool.wait_ge(norms_ready, a + 1)
                    pool.wait_ge(summed, a + 1)
                    pool.wait_ge(qk_projected, a)
                    nc.gpsimd.tensor_tensor(rot[:].rearrange("p t (h d) -> p (t h) d", d=hs),
                                            both[:].rearrange("p t (h d) -> p (t h) d", d=hs),
                                            along(norms[:], hs), ALU.mult).then_inc(rotated, 1)

                def start():
                    load_w(0, 0)
                    if rotary:
                        for a in range(3):
                            norm_factors(a, a)

                def group(g, half, first):
                    pool.wait_ge(out_ready, first + 1)
                    load_w(g + 1, 1 - half)

                def item(quad, p, buffers, b, gp):
                    if rotary:
                        norm_factors(quad * 4 + p + 3, p + 3)

                schedule(pool, start, item, group)
                for buffer in range(2):
                    pool.wait_ge(w_loaded[buffer], w_loads[buffer] * DMA)

            @block.tensor
            def _(pe):
                def project_rows(a, quad, p, wb):
                    pe.wait_ge(x_loaded[p], (quad + 1) * DMA)
                    pe.wait_ge(rows_ready, a)
                    for t in range(2):
                        last = nc.tensor.matmul(rows_p[:, t * 2 * P:(t + 1) * 2 * P], x[p][:, tile_of(t)],
                                                w[wb][:, 0:2 * P], start=True, stop=True)
                    last.then_inc(projected, 1)

                def project_qk(a, quad, p, wb):
                    if rotary:
                        pe.wait_ge(rotated, a + 1)
                        pe.wait_ge(qk_ready, a)
                        for n in range(2):
                            for t in range(2):
                                last = nc.tensor.transpose(qk_p[:, (2 * n + t) * P:(2 * n + t + 1) * P],
                                                           rot[:, t, tile_of(n)], core.ident[:])
                        last.then_inc(qk_projected, 1)
                    else:
                        pe.wait_ge(x_loaded[p], (quad + 1) * DMA)
                        pe.wait_ge(qk_ready, a)
                        for n in range(2):
                            last = nc.tensor.matmul(qk_p[:, n * SEQ:(n + 1) * SEQ], w[wb][:, tile_of(n)], x[p][:],
                                                    start=True, stop=True)
                        last.then_inc(qk_projected, 1)

                def project_v(a, p, wb):
                    pe.wait_ge(v_ready, a)
                    for t in range(2):
                        last = nc.tensor.matmul(v_p[:, tile_of(t)], x[p][:, tile_of(t)], w[wb][:, 2 * P:3 * P],
                                                start=True, stop=True)
                    last.then_inc(v_projected, 1)

                def scores(item_b, item_a, p, j, first=False):
                    if j == 0:
                        pe.wait_ge(qk_ready, item_a + 1)
                    if not first and heads > 1:
                        pe.wait_ge(max_ready if masked else exp_done, item_b * heads + j - 1)
                    bank = scores_p[buffer(p, j)]
                    rows_of_head = slice(product_rows * (j // shared), product_rows * (j // shared + 1))
                    for t in range(2):
                        k0, k1 = keys[t]
                        queries = qk[p % 2][rows_of_head, tile_of(2 * (j % shared) + t)]
                        last = nc.tensor.matmul(bank[:, t * SEQ + k0:t * SEQ + k1], queries,
                                                qk[p % 2][rows_of_head, keys_at + k0:keys_at + k1], start=True,
                                                stop=True)
                    last.then_inc(scores_ready, 1)

                def turn(item_c, item_b, p, j):
                    pe.wait_ge(probs_ready, item_b * heads + j + 1)
                    for n, (kt, qt) in enumerate(blocks):
                        last = nc.tensor.transpose(turned_p[buffer(p, j)][:, tile_of(n)], probs[p % 2][j][:, qt, tile_of(kt)],
                                                   core.ident[:])
                    last.then_inc(probs_turned, 1)

                def weigh(item_c, item_a, p, j):
                    if j == 0:
                        pe.wait_ge(v_ready, item_a + 1)
                        pe.wait_ge(added, item_c + 1)
                    pe.wait_ge(probs_t_ready, item_c * heads + j + 1)
                    of_head = slice(hs * j, hs * (j + 1))
                    pt = probs_t[buffer(p, j)]
                    nc.tensor.matmul(out_p[of_head, 0:SEQ], v[p % 2][:, 0, of_head], pt[:, 0:SEQ], start=True, stop=False)
                    last = nc.tensor.matmul(out_p[of_head, late:SEQ], v[p % 2][:, 1, of_head], pt[:, SEQ:], start=False,
                                            stop=True)
                    if j == heads - 1:
                        last.then_inc(heads_done, 1)

                def output(item_c, wb):
                    pe.wait_ge(heads_ready, item_c + 1)
                    for t in range(2):
                        last = nc.tensor.matmul(out_p[:, SEQ + t * P:SEQ + (t + 1) * P], heads_t[:, tile_of(t)],
                                                w[wb][:, 3 * P:4 * P], start=True, stop=True)
                    last.then_inc(out_ready, 1)

                def start():
                    pe.wait_ge(w_loaded[0], DMA)
                    if rotary:
                        project_rows(0, 0, 0, 0)
                        project_rows(1, 0, 1, 0)
                    for a in range(2):
                        project_qk(a, 0, a, 0)
                        project_v(a, a, 0)
                    if rotary:
                        project_rows(2, 0, 2, 0)
                    for j in range(heads):
                        scores(0, 0, 0, j, first=j < 2)

                def item(quad, p, buffers, b, gp):
                    k, now = quad * 4 + p, buffers[0]
                    if now != buffers[ahead] and now == buffers[ahead - 1]:
                        loads = gp + 1 if buffers[ahead] else gp + 2
                        pe.wait_ge(w_loaded[buffers[ahead]], loads * DMA)
                    if rotary:
                        project_rows(k + 3, quad + (p + 3) // 4, (p + 3) % 4, buffers[3])
                    for pass_ in range(0, heads, 2):
                        pass_heads = range(pass_, min(pass_ + 2, heads))
                        for j in pass_heads:
                            turn(k, k, p, j)
                        for j in pass_heads:
                            scores(k + 1, k + 1, p + 1, j)
                        for j in pass_heads:
                            weigh(k, k, p, j)
                    project_qk(k + 2, quad + (p + 2) // 4, (p + 2) % 4, buffers[2])
                    project_v(k + 2, (p + 2) % 4, buffers[2])
                    output(k, now)

                schedule(pe, start, item)

            @block.scalar
            def _(act):
                def copy_qk(a, p):
                    act.wait_ge(qk_projected, a + 1)
                    if rotary:
                        nc.scalar.activation(qk[p % 2][:], qk_p[:], ACT.Copy).then_inc(qk_ready, 1)
                    else:
                        nc.scalar.activation(qk[p % 2][:, 0:SEQ], qk_p[:, 0:SEQ], ACT.Copy, scale=scale)
                        nc.scalar.activation(qk[p % 2][:, SEQ:], qk_p[:, SEQ:], ACT.Copy).then_inc(qk_ready, 1)

                def copy_v(a, p, after_c=None):
                    act.wait_ge(v_projected, a + 1)
                    if after_c is not None:
                        act.wait_ge(heads_done, after_c)
                    nc.scalar.activation(v[p % 2][:], v_p[:, 0:SEQ].rearrange("p (t d) -> p t d", t=2), ACT.Copy)\
                        .then_inc(v_ready, 1)

                def copy_rows(a, p):
                    act.wait_ge(projected, a + 1)
                    if began(a - 1):
                        act.wait_ge(sin_done, a - 1)
                    nc.scalar.activation(rows[p % 2][:], rows_p[:].rearrange("p (t n) -> p t n", t=2), ACT.Copy)\
                        .then_inc(rows_ready, 1)

                def square_rows(a, p):
                    act.wait_ge(rows_ready, a + 1)
                    if began(a):
                        act.wait_ge(squares_summed, a)
                    nc.scalar.activation(squares[:], rows[p % 2][:], ACT.Square).then_inc(squares_ready, 1)

                def copy_probs(item_c, p, j):
                    act.wait_ge(probs_turned, item_c * heads + j + 1)
                    nc.scalar.activation(probs_t[buffer(p, j)][:], turned_p[buffer(p, j)][:, 0:len(blocks) * P], ACT.Copy)\
                        .then_inc(probs_t_ready, 1)

                def exps(item_b, p, j):
                    act.wait_ge(max_ready, item_b * heads + j + 1)
                    for t in range(2):
                        k0, k1 = keys[t]
                        mine = probs[p % 2][j][:, t, k0:k1]
                        if masked:
                            src, sign = mine, -1.0
                        else:
                            src, sign = scores_p[buffer(p, j)][:, t * SEQ + k0:t * SEQ + k1], 1.0
                        last = nc.scalar.activation(mine, src, ACT.Exp, scale=sign, bias=neg_max[:, j, t:t + 1],
                                                    accum_out=sums[:, j, t:t + 1])
                    last.then_inc(exp_done, 1)

                def copy_heads(item_c):
                    act.wait_ge(heads_done, item_c + 1)
                    nc.scalar.activation(heads_t[:], out_p[:, 0:SEQ], ACT.Copy).then_inc(heads_ready, 1)

                def start():
                    for a in range(2):
                        if rotary:
                            copy_rows(a, a)
                            square_rows(a, a)
                        elif not biased:
                            copy_qk(a, a)
                            copy_v(a, a)
                    if rotary:
                        for a in range(2):
                            copy_qk(a, a)
                            copy_v(a, a)
                        copy_rows(2, 2)
                        square_rows(2, 2)
                    for j in range(heads):
                        exps(0, 0, j)

                def item(quad, p, buffers, b, gp):
                    k = quad * 4 + p
                    if rotary:
                        copy_rows(k + 3, p + 3)
                        for j in range(heads):
                            copy_probs(k, p, j)
                        square_rows(k + 3, p + 3)
                    for pass_ in range(0, heads, 2):
                        pass_heads = range(pass_, min(pass_ + 2, heads))
                        if copies_by_act and not rotary:
                            for j in pass_heads:
                                copy_probs(k, p, j)
                        for j in pass_heads:
                            if heads == 2 and j == 1:
                                copy_heads(k)
                            exps(k + 1, p + 1, j)
                    if heads != 2:
                        copy_heads(k)
                    if not biased:
                        copy_qk(k + 2, p)
                        copy_v(k + 2, p, k + 1)

                schedule(act, start, item)

            @block.vector
            def _(dve):
                if window:
                    for p in range(2):
                        for j in range(heads):
                            nc.vector.memset(probs[p % 2][j][:, 1, 0:P - WINDOW], 0.0)

                def biased_qk(a, p, wb):
                    dve.wait_ge(qk_projected, a + 1)
                    for n in range(shared):
                        by = scale if shared == 1 else core.scale_of_every_other[:, n:n + 1]
                        nc.vector.tensor_scalar(qk[p % 2][:, n * SEQ:(n + 1) * SEQ], qk_p[:, 0:SEQ],
                                                w[wb][:, 4 * P:4 * P + 1], by, ALU.add, ALU.mult)
                    nc.vector.tensor_scalar(qk[p % 2][:, keys_at:], qk_p[:, SEQ:], w[wb][:, 4 * P + 1:4 * P + 2], None,
                                            ALU.add).then_inc(qk_ready, 1)

                def biased_v(a, p, wb):
                    dve.wait_ge(v_projected, a + 1)
                    bias = w[wb][:, 4 * P + 2:5 * P + 2].unsqueeze(1).to_broadcast([P, 2, P])
                    nc.vector.tensor_tensor(v[p % 2][:], v_p[:, 0:SEQ].rearrange("p (t d) -> p t d", t=2), bias, ALU.add)\
                        .then_inc(v_ready, 1)

                def sum_squares(a):
                    dve.wait_ge(squares_ready, a + 1)
                    if began(a):
                        dve.wait_ge(norms_ready, a)
                    nc.vector.tensor_reduce(square_sums[:], squares[:].rearrange("p t (h d) -> p (t h) d", d=hs), AX,
                                            ALU.add).then_inc(squares_summed, 1)
                    dve.wait_ge(squares_summed, a + 1)
                    nc.vector.tensor_scalar(square_sums[:], square_sums[:], 1e-24, None, ALU.max).then_inc(sums_ready, 1)

                def times_cos(a, p):
                    dve.wait_ge(rows_ready, a + 1)
                    if began(a - 1):
                        dve.wait_ge(rotated, a - 1)
                    nc.vector.tensor_tensor(by_cos[p % 2][:], rows[p % 2][:], cos[:], ALU.mult)

                def times_sin(a, p):
                    if began(a):
                        dve.wait_ge(summed, a)
                    src, dst, table = (m[:].rearrange("p t (h s d) -> p (t h) s d", s=2, d=hs // 2)
                                       for m in (rows[p % 2], by_sin, sin))
                    for s in range(2):
                        last = nc.vector.tensor_tensor(dst[:, :, s, :], src[:, :, 1 - s, :], table[:, :, s, :], ALU.mult)
                    last.then_inc(sin_done, 1)

                def maxima(item_b, p, j):
                    dve.wait_ge(scores_ready, item_b * heads + j + 1)
                    if masked:
                        nc.vector.memset(waited[:, j:j + 1], 0.0)
                    for t in range(2):
                        k0, k1 = keys[t]
                        src = scores_p[buffer(p, j)][:, t * SEQ + k0:t * SEQ + k1]
                        if masked:
                            mask = (core.window_masks if window else core.causal_masks)[t]
                            last = nc.vector.tensor_tensor_reduce(probs[p % 2][j][:, t, k0:k1], src, mask, -1.0, -NEG * 10,
                                                                  ALU.add, ALU.min, neg_max[:, j, t:t + 1])
                        else:
                            last = nc.vector.tensor_reduce(neg_max[:, j, t:t + 1], src, AX, ALU.max, negate=True)
                    last.then_inc(max_ready, 1)

                def normalise_probs(item_b, p, j):
                    unit = item_b * heads + j
                    dve.wait_ge(exp_done, unit + 1)
                    nc.vector.reciprocal(inverse[:, j, :], sums[:, j, :]).then_inc(inverse_ready, 1)
                    dve.wait_ge(inverse_ready, unit + 1)
                    for t in range(2):
                        k0, k1 = keys[t]
                        last = nc.vector.tensor_scalar(probs[p % 2][j][:, t, k0:k1], probs[p % 2][j][:, t, k0:k1],
                                                       inverse[:, j, t:t + 1], None, ALU.mult)
                    last.then_inc(probs_ready, 1)

                def copy_probs(item_c, p, j):
                    dve.wait_ge(probs_turned, item_c * heads + j + 1)
                    nc.vector.tensor_copy(probs_t[buffer(p, j)][:], turned_p[buffer(p, j)][:, 0:len(blocks) * P])\
                        .then_inc(probs_t_ready, 1)

                def add_output(item_c, b):
                    dve.wait_ge(out_ready, item_c + 1)
                    mine = res[:, bass.ds(b * 2, 2), :]
                    nc.vector.tensor_tensor(mine, mine, out_p[:, SEQ:].rearrange("p (t d) -> p t d", t=2), ALU.add)\
                        .then_inc(added, 1)

                def start():
                    dve.sem_inc(added, 1)
                    for a in range(3 if rotary else 2):
                        if rotary:
                            times_cos(a, a)
                            sum_squares(a)
                            times_sin(a, a)
                        elif biased:
                            biased_qk(a, a, 0)
                            biased_v(a, a, 0)
                    for j in range(heads):
                        maxima(0, 0, j)
                        normalise_probs(0, 0, j)

                def item(quad, p, buffers, b, gp):
                    k = quad * 4 + p
                    if rotary:
                        times_cos(k + 3, p + 3)
                        for j in range(heads):
                            maxima(k + 1, p + 1, j)
                        sum_squares(k + 3)
                        normalise_probs(k + 1, p + 1, 0)
                        times_sin(k + 3, p + 3)
                        normalise_probs(k + 1, p + 1, 1)
                        add_output(k, b)
                        return
                    for pass_ in range(0, heads, 2):
                        pass_heads = range(pass_, min(pass_ + 2, heads))
                        if not copies_by_act:
                            for j in pass_heads:
                                copy_probs(k, p, j)
                        for j in pass_heads:
                            maxima(k + 1, p + 1, j)
                        for j in pass_heads:
                            normalise_probs(k + 1, p + 1, j)
                    if biased:
                        biased_qk(k + 2, p, buffers[2])
                        dve.wait_ge(heads_done, k + 1)
                        biased_v(k + 2, p, buffers[2])
                    add_output(k, b)

                schedule(dve, start, item)


@as_stage
def feed_forward(core, name, w_dram, src_t, res, experts, parts, func, gated=False, biased=False, shares=None, layer=0):
    nc, E, C, H = core.nc, experts, CHUNKS, parts
    ups = H * P if gated else 0
    w2_at = (2 * H if gated else H) * P
    b1_at = w2_at + H * P
    b2_at = b1_at + (2 * H if gated else H)
    halves = min(E, 2)
    w_loads = (E // 2 + 1, max(E // 2, 1))
    in_flight = 2 if gated else 4

    w_loaded = core.sems(name, "w_loaded0", "w_loaded1")
    y_added = core.sems(name, "y_added0", "y_added1")
    hidden_psum, gate_ready, hidden_ready, y_ready = core.sems(name, "hidden_psum", "gate_ready", "hidden_ready", "y_ready")

    with ExitStack() as ctx:
        def sb(n, shape, dt=F32):
            return ctx.enter_context(nc.sbuf_tensor(f"{name}_{n}", shape, dt))

        w = [sb(f"w{i}", [P, w_dram.shape[2]]) for i in range(2)]
        hidden = [sb(f"hidden{i}", [P, H, CHUNK]) for i in range(2)]
        gate = [sb(f"gate{i}", [P, CHUNK]) for i in range(2)] if gated else None

        def unit_banks(p, h):
            u = (p * H + h) % in_flight
            return core.banks[2 * u:2 * u + 2] if gated else core.banks[u:u + 1]

        def gate_of(p, h):
            return gate[(p * H + h) % 2]

        y_p = core.banks[4:6]

        def schedule(eng, start, item, expert=None):
            start()

            def expert_pair(ep):
                for half in range(halves):
                    pair = ep * C + half * (C // 2)
                    e = ep * 2 + half
                    if expert:
                        expert(e, half, pair * 2)
                    with eng.Fori(0, C // 2 - 1) as i:
                        for p in range(2):
                            item(pair + i, p, half, half, i * 2 + p, i * 2 + p + 1, e, ep)
                    for p in range(2):
                        item(pair + C // 2 - 1, p, half, half if p == 0 else 1 - half, C - 2 + p, (C - 1 + p) % C, e, ep)

            if E > 2:
                with eng.Fori(0, E // 2) as ep:
                    expert_pair(ep)
            else:
                expert_pair(0)

        with nc.Block() as block:
            @block.sync
            def _(sp):
                def load_w(e, buffer):
                    src = w_dram[bass.ds(layer * E + e, 1), :, :].rearrange("a p n -> p (a n)")
                    sp.dma_start(w[buffer][:], src).then_inc(w_loaded[buffer], DMA)

                def start():
                    load_w(0, 0)

                def expert(e, half, first):
                    sp.wait_ge(y_ready, first + 1)
                    load_w(e + 1, 1 - half)

                schedule(sp, start, lambda *a: None, expert)
                for buffer in range(2):
                    sp.wait_ge(w_loaded[buffer], w_loads[buffer] * DMA)

            @block.tensor
            def _(pe):
                def hide(item_h, p, wb, c, first=False):
                    for h in range(H):
                        if not (first and h < in_flight) and h + 1 + H > in_flight:
                            pe.wait_ge(hidden_ready, item_h * H + h + 1 - in_flight)
                        for n, bank in enumerate(unit_banks(p, h)):
                            at = n * ups + h * P
                            last = nc.tensor.matmul(bank[:], w[wb][:, at:at + P], src_t[:, bass.ds(c * CHUNK, CHUNK)],
                                                    start=True, stop=True)
                        last.then_inc(hidden_psum, 1)

                def give(item_h, pair, p, wb):
                    pe.wait_ge(hidden_ready, (item_h + 1) * H)
                    pe.wait_ge(y_added[p], pair + 1)
                    for t in range(CHUNK // P):
                        for h in range(H):
                            last = nc.tensor.matmul(y_p[p][:, tile_of(t)], hidden[p][:, h, tile_of(t)],
                                                    w[wb][:, w2_at + h * P:w2_at + (h + 1) * P], start=h == 0,
                                                    stop=h == H - 1 and not biased)
                        if biased:
                            last = nc.tensor.matmul(y_p[p][:, tile_of(t)], core.ones[0:1, :], w[wb][0:1, b2_at:b2_at + P],
                                                    start=False, stop=True)
                    last.then_inc(y_ready, 1)

                def start():
                    pe.wait_ge(w_loaded[0], DMA)
                    hide(0, 0, 0, 0, first=True)

                def item(pair, p, now, nxt, c, c_next, e, ep):
                    k = pair * 2 + p
                    if now != nxt:
                        loads = ep + 1 if nxt else ep + 2
                        pe.wait_ge(w_loaded[nxt], loads * DMA)
                    hide(k + 1, 1 - p, nxt, c_next)
                    give(k, pair, p, now)

                schedule(pe, start, item)

            @block.scalar
            def _(act):
                def activate(item_h, p, wb):
                    for h in range(H):
                        act.wait_ge(hidden_psum, item_h * H + h + 1)
                        bias = {"bias": w[wb][:, b1_at + h:b1_at + h + 1]} if biased else {}
                        dst = gate_of(p, h)[:] if gated else hidden[p][:, h, :]
                        nc.scalar.activation(dst, unit_banks(p, h)[0][:], func, **bias)\
                            .then_inc(gate_ready if gated else hidden_ready, 1)

                def start():
                    activate(0, 0, 0)

                def item(pair, p, now, nxt, c, c_next, e, ep):
                    activate(pair * 2 + p + 1, 1 - p, nxt)

                schedule(act, start, item)

            @block.vector
            def _(dve):
                def times_gate(item_h, p, wb):
                    for h in range(H):
                        dve.wait_ge(gate_ready, item_h * H + h + 1)
                        up, dst = unit_banks(p, h)[1][:], hidden[p][:, h, :]
                        if biased:
                            bias = w[wb][:, b1_at + H + h:b1_at + H + h + 1]
                            last = nc.vector.scalar_tensor_tensor(dst, up, bias, gate_of(p, h)[:], ALU.add, ALU.mult)
                        else:
                            last = nc.vector.tensor_tensor(dst, up, gate_of(p, h)[:], ALU.mult)
                        last.then_inc(hidden_ready, 1)

                def start():
                    for p in range(2):
                        dve.sem_inc(y_added[p], 1)
                    if gated:
                        times_gate(0, 0, 0)

                def item(pair, p, now, nxt, c, c_next, e, ep):
                    k = pair * 2 + p
                    if gated:
                        times_gate(k + 1, 1 - p, nxt)
                    dve.wait_ge(y_ready, k + 1)
                    tiles = CHUNK // P
                    if shares is None:
                        mine = res[:, bass.ds(c * tiles, tiles), :]
                        last = nc.vector.tensor_tensor(mine, mine, y_p[p][:].rearrange("p (t d) -> p t d", t=tiles), ALU.add)
                    else:
                        for t in range(tiles):
                            mine = res[:, bass.ds(c * tiles + t, 1), :].rearrange("p a d -> p (a d)")
                            share = shares[:, bass.ds(e * TILES + c * tiles + t, 1)]
                            last = nc.vector.scalar_tensor_tensor(mine, y_p[p][:, tile_of(t)], share, mine, ALU.mult, ALU.add)
                    last.then_inc(y_added[p], 1)

                schedule(dve, start, item)


def find_slots(nc, selected, slots, numbers, b):
    capacity, n = numbers.shape[1], 2 * EXPERTS
    return nc.vector.tensor_tensor(selected[:].rearrange("p (n s) -> p n s", n=n), along(slots[:, b * n:(b + 1) * n], capacity),
                                   numbers.unsqueeze(1).to_broadcast([P, n, capacity]), ALU.is_equal)


@as_stage
def dispatch(core, name, rows, slots, numbers, slots_t):
    nc, width = core.nc, EXPERTS * numbers.shape[1]
    selected_ready, dispatched, moved = core.sems(name, "selected_ready", "dispatched", "moved")
    with ExitStack() as ctx:
        selected = [ctx.enter_context(nc.sbuf_tensor(f"{name}_selected{i}", [P, 2 * width], F32)) for i in range(2)]
        with nc.Block() as block:
            @block.vector
            def _(dve):
                for b in range(BATCH):
                    if b >= 2:
                        dve.wait_ge(dispatched, b - 1)
                    find_slots(nc, selected[b % 2], slots, numbers, b).then_inc(selected_ready, 1)

            @block.tensor
            def _(pe):
                for b in range(BATCH):
                    pe.wait_ge(selected_ready, b + 1)
                    if b >= 4:
                        pe.wait_ge(moved, b - 3)
                    for t in range(2):
                        last = nc.tensor.matmul(core.banks[b % 4][:, 0:width], rows[:, 2 * b + t, :],
                                                selected[b % 2][:, t * width:(t + 1) * width], start=t == 0, stop=t == 1)
                    last.then_inc(dispatched, 1)

            @block.scalar
            def _(act):
                for b in range(BATCH):
                    act.wait_ge(dispatched, b + 1)
                    nc.scalar.activation(slots_t[:, b * width:(b + 1) * width], core.banks[b % 4][:, 0:width], ACT.Copy)\
                        .then_inc(moved, 1)


@as_stage
def feed_forward_of_slots(core, name, w_dram, slots_t, y_t, capacity, parts, func):
    nc, H, half_batches = core.nc, parts, BATCH // 2
    w2_at, b1_at, b2_at = H * P, 2 * H * P, 2 * H * P + H
    width = half_batches * capacity
    w_loaded = core.sems(name, "w_loaded0", "w_loaded1")
    y_moved = core.sems(name, "y_moved0", "y_moved1")
    hidden_psum, hidden_ready, y_ready = core.sems(name, "hidden_psum", "hidden_ready", "y_ready")
    with ExitStack() as ctx:
        w = [ctx.enter_context(nc.sbuf_tensor(f"{name}_w{i}", [P, w_dram.shape[2]], F32)) for i in range(2)]
        hidden = [ctx.enter_context(nc.sbuf_tensor(f"{name}_hidden{i}", [P, H, width], F32)) for i in range(2)]
        y_p = core.banks[4:6]

        def of_item(tensor, e, c):
            by_slot = tensor[:].rearrange("p (b e s) -> p b e s", e=EXPERTS, s=capacity)
            part = by_slot[:, c * half_batches:(c + 1) * half_batches, bass.ds(e, 1), :]
            return part.rearrange("p b a s -> p b (a s)")

        def by_batch(ap):
            return ap.rearrange("p (b s) -> p b s", s=capacity)

        def run(eng, start, item, expert=None):
            def expert_pair(ep, final):
                for half in range(2):
                    e = ep * 2 + half
                    if expert:
                        expert(e, half)
                    for c in range(2):
                        item(e * 2 + c, half, c, e, ep, final and half == 1 and c == 1)

            start()
            with eng.Fori(0, EXPERTS // 2 - 1) as ep:
                expert_pair(ep, False)
            expert_pair(EXPERTS // 2 - 1, True)

        with nc.Block() as block:
            @block.sync
            def _(sp):
                def load_w(e, buffer):
                    src = w_dram[bass.ds(e, 1), :, :].rearrange("a p n -> p (a n)")
                    sp.dma_start(w[buffer][:], src).then_inc(w_loaded[buffer], DMA)

                def expert(e, half):
                    sp.wait_ge(y_moved[1], e + 1)
                    load_w(e + 1, 1 - half)

                run(sp, lambda: load_w(0, 0), lambda *a: None, expert)
                sp.wait_ge(w_loaded[0], (EXPERTS // 2 + 1) * DMA)
                sp.wait_ge(w_loaded[1], EXPERTS // 2 * DMA)

            @block.tensor
            def _(pe):
                def hide(k, half, c, e, first=False):
                    for h in range(H):
                        if not first:
                            pe.wait_ge(hidden_ready, (k - 1) * H + h + 1)
                        nc.tensor.matmul(by_batch(core.banks[h][:, 0:width]), w[half][:, h * P:(h + 1) * P],
                                         of_item(slots_t, e, c), start=True, stop=True).then_inc(hidden_psum, 1)

                def start():
                    pe.wait_ge(w_loaded[0], DMA)
                    hide(0, 0, 0, 0, first=True)

                def item(k, half, c, e, ep, final):
                    if c == 0:
                        hide(k + 1, half, 1, e)
                    elif not final:
                        pe.wait_ge(w_loaded[1 - half], (ep + 1 if half == 0 else ep + 2) * DMA)
                        hide(k + 1, 1 - half, 0, e + 1)
                    pe.wait_ge(hidden_ready, (k + 1) * H)
                    pe.wait_ge(y_moved[c], e + 1)
                    for h in range(H):
                        last = nc.tensor.matmul(y_p[c][:, 0:width], w[half][:, w2_at + h * P:w2_at + (h + 1) * P],
                                                hidden[c][:, h, :], start=h == 0, stop=h == H - 1)
                    last.then_inc(y_ready, 1)

                run(pe, start, item)

            @block.scalar
            def _(act):
                def item(k, half, c, e, ep, final):
                    for h in range(H):
                        act.wait_ge(hidden_psum, k * H + h + 1)
                        nc.scalar.activation(hidden[c][:, h, :], core.banks[h][:, 0:width], func,
                                             bias=w[half][:, b1_at + h:b1_at + h + 1]).then_inc(hidden_ready, 1)

                run(act, lambda: None, item)

            @block.vector
            def _(dve):
                def start():
                    for c in range(2):
                        dve.sem_inc(y_moved[c], 1)

                def item(k, half, c, e, ep, final):
                    dve.wait_ge(y_ready, k + 1)
                    nc.vector.tensor_scalar(of_item(y_t, e, c), by_batch(y_p[c][:, 0:width]), w[half][:, b2_at:b2_at + 1],
                                            None, ALU.add).then_inc(y_moved[c], 1)

                run(dve, start, item)


@as_stage
def combine(core, name, y_t, slots, numbers, shares, res):
    nc, capacity = core.nc, numbers.shape[1]
    width = EXPERTS * capacity
    groups = [(at, min(at + 3 * capacity, width)) for at in range(0, width, 3 * capacity)]
    most, rest = groups[0][1], groups[2][1] - groups[2][0]
    selected_ready, weighted_ready, turned, act_copied, dve_copied, combined, added = core.sems(
        name, "selected_ready", "weighted_ready", "turned", "act_copied", "dve_copied", "combined", "added")
    with ExitStack() as ctx:
        def pair(n, shape):
            return [ctx.enter_context(nc.sbuf_tensor(f"{name}_{n}{i}", shape, F32)) for i in range(2)]

        selected, weighted = pair("selected", [P, 2 * width]), pair("weighted", [P, 2 * width])
        shares_t, last_group, y_rows = pair("shares_t", [P, 2 * SEQ]), pair("last_group", [P, SEQ + P]), pair("y_rows", [P, 2 * P])
        with nc.Block() as block:
            @block.vector
            def _(dve):
                def find(b):
                    if b >= 2:
                        dve.wait_ge(weighted_ready, b - 1)
                    find_slots(nc, selected[b % 2], slots, numbers, b).then_inc(selected_ready, 1)

                find(0)
                find(1)
                for b in range(BATCH):
                    dve.wait_ge(turned, b + 1)
                    if b >= 2:
                        dve.wait_ge(combined, b - 1)
                    nc.vector.tensor_copy(y_rows[b % 2][0:most, :], core.banks[b % 2 * 3 + 2][0:most, 0:2 * P])\
                        .then_inc(dve_copied, 1)
                    if b + 2 < BATCH:
                        find(b + 2)
                    dve.wait_ge(combined, b + 1)
                    mine = res[:, 2 * b:2 * b + 2, :]
                    nc.vector.tensor_tensor(mine, mine, core.banks[6 + b % 2][:, 0:2 * D].rearrange("p (t d) -> p t d", t=2),
                                            ALU.add).then_inc(added, 1)

            @block.gpsimd
            def _(pool):
                for b in range(BATCH):
                    pool.wait_ge(selected_ready, b + 1)
                    if b >= 2:
                        pool.wait_ge(turned, b - 1)
                    n = 2 * EXPERTS
                    nc.gpsimd.tensor_tensor(weighted[b % 2][:].rearrange("p (n s) -> p n s", n=n),
                                            selected[b % 2][:].rearrange("p (n s) -> p n s", n=n),
                                            along(shares[:, b * n:(b + 1) * n], capacity), ALU.mult)\
                        .then_inc(weighted_ready, 1)

            @block.tensor
            def _(pe):
                def turn(b):
                    pe.wait_ge(weighted_ready, b + 1)
                    if b >= 2:
                        pe.wait_ge(act_copied, b - 1)
                        pe.wait_ge(dve_copied, b - 1)
                    by_share, by_rest, by_y = core.banks[b % 2 * 3:b % 2 * 3 + 3]
                    for g, (at, end) in enumerate(groups):
                        for t in range(2):
                            bank, n = (by_rest, t) if g == 2 else (by_share, 2 * g + t)
                            nc.tensor.transpose(bank[0:end - at, tile_of(n)],
                                                weighted[b % 2][:, t * width + at:t * width + end], core.ident[:])
                        bank, n = (by_rest, 2) if g == 2 else (by_y, g)
                        last = nc.tensor.transpose(bank[0:end - at, tile_of(n)], y_t[:, b * width + at:b * width + end],
                                                   core.ident[:])
                    last.then_inc(turned, 1)

                turn(0)
                for b in range(BATCH):
                    if b + 1 < BATCH:
                        turn(b + 1)
                    pe.wait_ge(act_copied, b + 1)
                    pe.wait_ge(dve_copied, b + 1)
                    if b >= 2:
                        pe.wait_ge(added, b - 1)
                    for t in range(2):
                        out = core.banks[6 + b % 2][:, tile_of(t)]
                        for g in range(2):
                            nc.tensor.matmul(out, shares_t[b % 2][0:most, tile_of(2 * g + t)], y_rows[b % 2][0:most, tile_of(g)],
                                             start=g == 0, stop=False)
                        last = nc.tensor.matmul(out, last_group[b % 2][0:rest, tile_of(t)], last_group[b % 2][0:rest, tile_of(2)],
                                                start=False, stop=True)
                    last.then_inc(combined, 1)

            @block.scalar
            def _(act):
                for b in range(BATCH):
                    act.wait_ge(turned, b + 1)
                    if b >= 2:
                        act.wait_ge(combined, b - 1)
                    by_share, by_rest = core.banks[b % 2 * 3:b % 2 * 3 + 2]
                    nc.scalar.activation(shares_t[b % 2][0:most, :], by_share[0:most, :], ACT.Copy)
                    nc.scalar.activation(last_group[b % 2][0:rest, :], by_rest[0:rest, 0:SEQ + P], ACT.Copy)\
                        .then_inc(act_copied, 1)


def router_logits(core, pe, src_t, wr, n, bank, done):
    for t in range(TILES):
        last = core.nc.tensor.matmul(bank[:, t * n:(t + 1) * n], src_t[:, tile_of(t)], wr[:, 0:n], start=True, stop=True)
    last.then_inc(done, 1)


def by_expert(tensor, n):
    return tensor[:, 0:TILES * n].rearrange("p (t e) -> p t e", e=n)


def first_best(nc, link, values, is_best, best, scratch, at_best, earliest, n):
    link(nc.vector.tensor_reduce(best[:], by_expert(values, n), AX, ALU.max))
    link(nc.vector.tensor_tensor(by_expert(scratch, n), by_expert(values, n), along(best[:], n), ALU.is_equal))
    link(nc.vector.tensor_tensor(scratch[:], scratch[:], earliest[:], ALU.mult))
    link(nc.vector.tensor_reduce(at_best[:], by_expert(scratch, n), AX, ALU.max))
    link(nc.vector.tensor_tensor(by_expert(is_best, n), by_expert(scratch, n), along(at_best[:], n), ALU.is_equal))


@as_stage
def route_top2(core, name, src_t, wr, shares, slots=None, capacity=None, chunk=None):
    nc, n = core.nc, 8
    cols = TILES * n
    logits_ready, exp_in, exp_done, chosen_ready, counted, chained = core.sems(
        name, "logits_ready", "exp_in", "exp_done", "chosen_ready", "counted", "chained")
    with ExitStack() as ctx:
        def sb(nm, width):
            return ctx.enter_context(nc.sbuf_tensor(f"{name}_{nm}", [P, width], F32))

        value, first, second, scratch, weight, chosen, rank, spare = (
            sb(nm, cols) for nm in ("value", "first", "second", "scratch", "weight", "chosen", "rank", "spare"))
        best, best2, at_best, total, low = (sb(nm, TILES) for nm in ("best", "best2", "at_best", "total", "low"))
        offsets = [sb(f"offsets{i}", n) for i in range(2)]
        logits_p, before_p, tile_p = core.banks[0][:, 0:cols], core.banks[1], core.banks[2]

        with nc.Block() as block:
            @block.tensor
            def _(pe):
                router_logits(core, pe, src_t, wr, n, core.banks[0], logits_ready)
                pe.wait_ge(chosen_ready, 1)
                last = nc.tensor.matmul(before_p[:, 0:cols], core.is_before[:], chosen[:], start=True, stop=capacity is None)
                if capacity is not None:
                    halves = before_p[:, 0:cols].rearrange("p (b t e) -> p b t e", t=2, e=n)
                    firsts = chosen[:].rearrange("p (b t e) -> p b t e", t=2, e=n)
                    last = nc.tensor.matmul(halves[:, :, 1, :], core.ones[:], firsts[:, :, 0, :], start=False, stop=True)
                else:
                    last = nc.tensor.matmul(tile_p[:, 0:cols], core.ones[:], chosen[:], start=True, stop=True)
                last.then_inc(counted, 1)

            @block.scalar
            def _(act):
                act.wait_ge(exp_in, 1)
                if capacity is not None:
                    nc.scalar.activation(value[:], value[:], ACT.Exp).then_inc(exp_done, 1)
                else:
                    nc.scalar.activation(low[:], low[:], ACT.Exp).then_inc(exp_done, 1)

            @block.vector
            def _(dve):
                link = chain(dve, chained)
                v = nc.vector

                def add_weighted(out, choice, w):
                    link(v.tensor_tensor(by_expert(out, n), by_expert(choice, n), along(w[:], n), ALU.mult))

                dve.wait_ge(logits_ready, 1)
                link(v.tensor_copy(value[:], logits_p))
                if capacity is not None:
                    link(v.tensor_reduce(best[:], by_expert(value, n), AX, ALU.max))
                    v.tensor_tensor(by_expert(value, n), by_expert(value, n), along(best[:], n), ALU.subtract)\
                        .then_inc(exp_in, 1)
                    dve.wait_ge(exp_done, 1)
                    link(v.tensor_reduce(total[:], by_expert(value, n), AX, ALU.add))
                    link(v.reciprocal(total[:], total[:]))
                    link(v.tensor_tensor(by_expert(value, n), by_expert(value, n), along(total[:], n), ALU.mult))
                first_best(nc, link, value, first, best, scratch, at_best, core.earliest, n)
                link(v.scalar_tensor_tensor(spare[:], first[:], NEG, value[:], ALU.mult, ALU.add))
                first_best(nc, link, spare, second, best2, scratch, at_best, core.earliest, n)
                v.tensor_tensor(chosen[:], first[:], second[:], ALU.add).then_inc(chosen_ready, 1)
                if capacity is not None:
                    dve.wait_ge(counted, 1)
                    link(v.scalar_tensor_tensor(weight[:], before_p[:, 0:cols], float(capacity), chosen[:], ALU.is_lt,
                                                ALU.mult))
                    link(v.scalar_tensor_tensor(slots[:], before_p[:, 0:cols], 1.0, weight[:], ALU.add, ALU.mult))
                    link(v.tensor_tensor(shares[:, 0:cols], weight[:], value[:], ALU.mult))
                    return
                v.tensor_tensor(low[:], best2[:], best[:], ALU.subtract).then_inc(exp_in, 1)
                dve.wait_ge(exp_done, 1)
                link(v.tensor_scalar(total[:], low[:], 1.0, None, ALU.add))
                link(v.reciprocal(total[:], total[:]))
                link(v.tensor_tensor(low[:], low[:], total[:], ALU.mult))
                add_weighted(weight, first, total)
                add_weighted(scratch, second, low)
                link(v.tensor_tensor(weight[:], weight[:], scratch[:], ALU.add))
                dve.wait_ge(counted, 1)
                link(v.tensor_copy(spare[:], tile_p[:, 0:cols]))
                have, other, step = spare, scratch, n
                while step < cols:
                    link(v.tensor_copy(other[:, 0:step], have[:, 0:step]))
                    link(v.tensor_tensor(other[:, step:], have[:, step:], have[:, 0:cols - step], ALU.add))
                    have, other, step = other, have, 2 * step
                link(v.tensor_tensor(rank[:], have[:], tile_p[:, 0:cols], ALU.subtract))
                link(v.tensor_tensor(rank[:], rank[:], before_p[:, 0:cols], ALU.add))
                link(v.memset(offsets[0][:], 0.0))
                link(v.tensor_copy(offsets[0][:, 1:n], have[:, cols - n:cols - 1]))
                step = 1
                have, other = offsets
                while step < n:
                    link(v.tensor_copy(other[:, 0:step], have[:, 0:step]))
                    link(v.tensor_tensor(other[:, step:], have[:, step:], have[:, 0:n - step], ALU.add))
                    have, other, step = other, have, 2 * step
                link(v.tensor_tensor(by_expert(rank, n), by_expert(rank, n),
                                     have[:].unsqueeze(1).to_broadcast([P, TILES, n]), ALU.add))
                link(v.tensor_scalar(spare[:], rank[:], float(chunk), None, ALU.is_ge))
                for c in range(2, n):
                    link(v.scalar_tensor_tensor(spare[:], rank[:], float(c * chunk), spare[:], ALU.is_ge, ALU.add))
                for c in range(n):
                    link(v.scalar_tensor_tensor(scratch[:], spare[:], float(c), weight[:], ALU.is_equal, ALU.mult))
                    link(v.tensor_reduce(shares[:, c * TILES:(c + 1) * TILES], by_expert(scratch, n), AX, ALU.add))


@as_stage
def route_top8(core, name, src_t, wr, bias, shares, route_scale):
    nc, n = core.nc, 16
    cols = TILES * n
    logits_ready, scores_ready, chained = core.sems(name, "logits_ready", "scores_ready", "chained")
    with ExitStack() as ctx:
        def sb(nm, width):
            return ctx.enter_context(nc.sbuf_tensor(f"{name}_{nm}", [P, width], F32))

        score, select, left, top = sb("score", cols), sb("select", cols), sb("left", cols), sb("top", TILES * 8)
        total = sb("total", TILES)
        with nc.Block() as block:
            @block.tensor
            def _(pe):
                router_logits(core, pe, src_t, wr, n, core.banks[0], logits_ready)

            @block.scalar
            def _(act):
                act.wait_ge(logits_ready, 1)
                nc.scalar.activation(score[:], core.banks[0][:, 0:cols], ACT.Sigmoid).then_inc(scores_ready, 1)

            @block.vector
            def _(dve):
                link = chain(dve, chained)
                v = nc.vector
                dve.wait_ge(scores_ready, 1)
                link(v.tensor_tensor(by_expert(select, n), by_expert(score, n), bias.unsqueeze(1).to_broadcast([P, TILES, n]),
                                     ALU.add))
                for t in range(TILES):
                    link(v.max(top[:, t * 8:(t + 1) * 8], select[:, t * n:(t + 1) * n]))
                    link(v.match_replace(left[:, t * n:(t + 1) * n], top[:, t * 8:(t + 1) * 8],
                                         select[:, t * n:(t + 1) * n], NEG))
                link(v.scalar_tensor_tensor(left[:], left[:], NEG, score[:], ALU.is_equal, ALU.mult))
                link(v.tensor_reduce(total[:], by_expert(left, n), AX, ALU.add))
                link(v.reciprocal(total[:], total[:]))
                link(v.tensor_scalar(total[:], total[:], route_scale, None, ALU.mult))
                out = shares[:, 0:cols].rearrange("p (e t) -> p t e", t=TILES)
                link(v.tensor_tensor(out, by_expert(left, n), along(total[:], n), ALU.mult))


@as_stage
def load_rotary(core, base, src):
    (loaded,) = core.sems("rotary", "loaded")
    with core.nc.Block() as block:
        @block.sync
        def _(sp):
            sp.dma_start(base[:], src).then_inc(loaded, DMA)
            sp.wait_ge(loaded, DMA)


@as_stage
def rotary_tables(core, name, cos, sin, base, scales_dram, layer):
    nc = core.nc
    (loaded,) = core.sems(name, "loaded")
    with ExitStack() as ctx:
        scales = ctx.enter_context(nc.sbuf_tensor(f"{name}_scales", [P, 2, 2 * P], F32))
        with nc.Block() as block:
            @block.sync
            def _(sp):
                src = scales_dram[bass.ds(layer, 1), :].rearrange("a n -> (a n)").partition_broadcast(P)
                sp.dma_start(scales[:].rearrange("p a n -> p (a n)"), src).then_inc(loaded, DMA)

            @block.vector
            def _(dve):
                dve.wait_ge(loaded, DMA)
                for n, table in enumerate((cos, sin)):
                    nc.vector.tensor_tensor(table[:], base[:, n], scales[:, n, :].unsqueeze(1).to_broadcast([P, 2, 2 * P]),
                                            ALU.mult)


def build(nc, t, out, upto=99):
    with ExitStack() as ctx:
        core = Core(nc, ctx)
        res = core.keep("residual", [P, TILES, D])
        xn_t = core.keep("normed_t", [P, TOKENS])
        core.ident, core.is_before, core.ones = (core.keep(n, [P, P]) for n in ("ident", "is_before", "ones"))
        core.scale_of_every_other = core.keep("scale_of_every_other", [P, 2])
        core.minus_half = core.keep("minus_half", [P, TILES])
        core.earliest = core.keep("earliest", [P, TILES * 8])
        masks = core.keep("masks", [P, 4 * P + WINDOW])
        core.causal_masks = masks[:, P:2 * P], masks[:, 0:2 * P]
        core.window_masks = masks[:, 2 * P:3 * P], masks[:, 3 * P:4 * P + WINDOW]
        shares = core.keep("shares", [P, TILES * 16])
        wr0, wr1, wr3 = core.keep("wr0", [P, 8]), core.keep("wr1", [P, 16]), core.keep("wr3", [P, 8])
        slot_numbers = core.keep("slot_numbers", [P, CAPACITY])
        bo0, bo3, bias1 = core.keep("bo0", [P, D]), core.keep("bo3", [P, D]), core.keep("bias1", [P, 16])

        def rows(name):
            return t[name].partition_broadcast(P)

        load(core, [(res[:], t["x"].rearrange("b (t p) d -> p (b t) d", p=P)), (core.ident[:], t["ident"]),
                    (core.is_before[:], t["is_before"]), (core.earliest[:], rows("earliest")), (masks[:], t["masks"]),
                    (slot_numbers[:], rows("slot_numbers")),
                    (core.scale_of_every_other[:], t["scale_of_every_other"]),
                    (wr0[:], t["wr0"]), (wr1[:], t["wr1"]), (wr3[:], t["wr3"]), (bo0[:], rows("bo0")),
                    (bo3[:], rows("bo3")), (bias1[:], rows("bias1"))])

        if 0 < upto < 20 or upto > 30:
            with ExitStack() as block0:
                rows0, slots = (block0.enter_context(nc.sbuf_tensor(n, shape, F32))
                                for n, shape in (("rows0", [P, TILES, D]), ("slots", [P, TILES * EXPERTS])))
                normalise(core, "n0", res, xn_t, rows=rows0)
                route_top2(core, "r0", xn_t, wr0, shares, slots=slots, capacity=CAPACITY)
                if upto != 11:
                    add_row(core, "b0", res, bo0[:])
                    attention(core, "a0", t["a0"], xn_t, res, groups=8, heads=2, scale=64 ** -0.5)
                if upto != 10:
                    slots_t, y0_t = (block0.enter_context(nc.sbuf_tensor(n, [P, BATCH * EXPERTS * CAPACITY], F32))
                                     for n in ("slots_t", "y0_t"))
                    dispatch(core, "d0", rows0, slots, slot_numbers[:], slots_t)
                    feed_forward_of_slots(core, "f0", t["f0"], slots_t, y0_t, CAPACITY, 4, ACT.Relu)
                    combine(core, "c0", y0_t, slots, slot_numbers[:], shares, res)
        if 1 < upto < 10 or upto > 30 or upto == 22:
            normalise(core, "n1", res, xn_t)
            route_top8(core, "r1", xn_t, wr1, bias1[:], shares, 2.826)
            attention(core, "a1", t["a1"], xn_t, res, groups=8, heads=2, causal=True, scale=64 ** -0.5)
            feed_forward(core, "f1", t["f1"], xn_t, res, 16, 1, ACT.Silu, gated=True, shares=shares)
            feed_forward(core, "f1s", t["f1s"], xn_t, res, 1, 1, ACT.Silu, gated=True)
        if 2 < upto < 10 or upto > 30 or upto == 20:
            with ExitStack() as inner:
                y = inner.enter_context(nc.sbuf_tensor("inner", [P, TILES, D], F32))
                y_t = inner.enter_context(nc.sbuf_tensor("inner_t", [P, TOKENS], F32))
                base = inner.enter_context(nc.sbuf_tensor("rotary", [P, 2, 2, 2 * P], F32))
                cos, sin = (inner.enter_context(nc.sbuf_tensor(n, [P, 2, 2 * P], F32)) for n in ("cos", "sin"))
                normalise(core, "n2", res, xn_t, rows=y)
                load_rotary(core, base, t["rotary"])
                attention(core, "a2", t["a2"], xn_t, res, groups=1, heads=1, causal=True, scale=float(D) ** -0.5,
                          biased=True)
                with nc.Fori(0, DEPTH) as layer:
                    rotary_tables(core, "t2", cos, sin, base, t["qk_scales"], layer)
                    transpose_shifted(core, "s2", y, y_t)
                    attention(core, "w2", t["w2"], y_t, y, groups=8, heads=2, window=True, rotary=(cos, sin), layer=layer)
                    normalise(core, "m2", y, y_t, gain_bias=t["gain_bias"], layer=layer)
                    feed_forward(core, "f2", t["f2"], y_t, y, 1, 3, ACT.Gelu, gated=True, biased=True, layer=layer)
                add_rows(core, res, y)
        if 3 < upto < 10 or upto > 30 or upto == 21:
            normalise(core, "n3", res, xn_t)
            route_top2(core, "r3", xn_t, wr3, shares, chunk=TOKENS * 2 // 8)
            add_row(core, "b3", res, bo3[:])
            attention(core, "a3", t["a3"], xn_t, res, groups=4, heads=4, scale=8 ** -0.5, biased=True)
            feed_forward(core, "f3", t["f3"], xn_t, res, 8, 4, ACT.Gelu, shares=shares)
        store(core, res, out)


def constants():
    i = np.arange(P)
    late = np.arange(P + WINDOW)
    masks = [np.zeros((P, P)), np.where(i[None, :] <= i[:, None], 0.0, NEG),
             np.where((i[None, :] <= i[:, None]) & (i[None, :] >= i[:, None] - WINDOW), 0.0, NEG),
             np.where((late[None, :] >= i[:, None]) & (late[None, :] <= i[:, None] + WINDOW), 0.0, NEG)]
    half = np.arange(0, 64, 2, dtype=np.float32)
    freqs = np.arange(SEQ, dtype=np.float32)[:, None] * (1.0 / 10000.0 ** (half / np.float32(64)))[None, :]
    freqs = np.concatenate([freqs, freqs], -1).astype(np.float32)
    power = (np.arange(SEQ, dtype=np.float32) - SEQ // 2) / (WINDOW // 2)
    scale = ((half + 0.4 * 64) / (1.4 * 64))[None, :].astype(np.float32) ** power[:, None]
    scale = np.concatenate([scale, scale], -1).astype(np.float32)
    sign = np.where(np.arange(64) < 32, -1.0, 1.0)
    tables = np.empty((2, SEQ, 2, 2, 64), np.float32)
    for n, turn in enumerate((np.cos(freqs), np.sin(freqs) * sign)):
        tables[n, :, 0] = (8.0 * turn * scale)[:, None]
        tables[n, :, 1] = (turn / scale)[:, None]
    rotary = tables.reshape(2, 2, P, 2 * P).transpose(2, 0, 1, 3)
    return {
        "scale_of_every_other": 8 ** -0.5 * (i[:, None] // 32 % 2 == np.arange(2)),
        "slot_numbers": np.arange(CAPACITY) + 1,
        "ident": np.eye(P), "is_before": i[:, None] < i[None, :], "masks": np.concatenate(masks, 1),
        "earliest": np.tile(8 - np.arange(8), TILES), "rotary": rotary,
    }


def beside(*parts):
    return np.concatenate(parts, axis=-1)


def first_row(row):
    block = np.zeros((P, row.shape[-1]), np.float32)
    block[0] = row
    return block


def in_parts(w2):
    return w2.reshape(-1, P, w2.shape[-1]).transpose(1, 0, 2).reshape(P, -1)


def padded(groups):
    return np.stack(groups + [np.zeros_like(groups[0])])


def lay_out(i):
    def heads_of_two(q, k, v, o):
        return [beside(q[:, s], k[:, s], v[:, s], o[s, :]) for s in (slice(g * P, (g + 1) * P) for g in range(8))]

    def spread(m):
        wide = np.zeros(m.shape[:-1] + (4, 4, 32), np.float32)
        wide[..., :8] = m.reshape(m.shape[:-1] + (4, 4, 8))
        return [wide[..., g, :, :].reshape(m.shape[:-1] + (P,)) for g in range(4)]

    def column(row):
        return row[:, None]

    def on_all(row):
        return np.broadcast_to(row, (P, row.shape[-1]))

    inner, t = 1024, constants()
    t["x"] = i["L0_attn_hidden_states"]
    wkv = i["L0_attn_Wkv"]
    t["a0"] = padded(heads_of_two(i["L0_attn_Wq"], wkv[:, :inner], wkv[:, inner:], i["L0_attn_Wo"]))
    t["bo0"], t["wr0"] = i["L0_attn_bo"], i["L0_ffn_Wr"]
    t["f0"] = padded([beside(i["L0_ffn_W1"][e], in_parts(i["L0_ffn_W2"][e]), i["L0_ffn_b1"][e].reshape(4, P).T,
                             i["L0_ffn_b2"][e][:, None]) for e in range(8)])
    w = i["L1_attn_W_qkv"]
    t["a1"] = padded(heads_of_two(w[:, :inner], w[:, inner:2 * inner], w[:, 2 * inner:], i["L1_attn_W_out"]))
    t["wr1"], t["bias1"] = i["L1_ffn_gate_w"].T, i["L1_ffn_expert_bias"]
    t["f1"] = padded([beside(i["L1_ffn_w_gate"][e].T, i["L1_ffn_w_up"][e].T, i["L1_ffn_w_down"][e].T) for e in range(16)])
    t["f1s"] = padded([beside(i["L1_ffn_shared_gate_w"].T, i["L1_ffn_shared_up_w"].T, i["L1_ffn_shared_down_w"].T)])
    t["a2"] = padded([beside(i["L2_attn_Wq"].T, i["L2_attn_Wk"].T, i["L2_attn_Wv"].T, np.eye(P, dtype=np.float32),
                             column(i["L2_attn_bq"]), column(i["L2_attn_bk"]), on_all(i["L2_attn_bv"]))])
    groups = []
    for n in range(DEPTH):
        w = i["L2_ffn_Wqkv"][n]
        groups += heads_of_two(w[:, :inner], w[:, inner:2 * inner], w[:, 2 * inner:], i["L2_ffn_Wo"][n])
    t["w2"] = padded(groups)
    qs, ks = i["L2_ffn_q_scale"], i["L2_ffn_k_scale"]
    turned = [np.concatenate([s[:, 32:], s[:, :32]], 1) for s in (qs, ks)]
    t["qk_scales"] = beside(qs, qs, ks, ks, turned[0], turned[0], turned[1], turned[1])
    t["gain_bias"] = np.stack([i["L2_ffn_ln_g"], i["L2_ffn_ln_b"]], -1)
    layers = []
    for n in range(DEPTH):
        w1 = np.zeros((2, P, 3 * P), np.float32)
        b1 = np.zeros((2, 3 * P), np.float32)
        hidden = i["L2_ffn_W2"].shape[1]
        for half, at in enumerate((hidden, 0)):
            w1[half, :, :hidden] = i["L2_ffn_W1"][n][:, at:at + hidden]
            b1[half, :hidden] = i["L2_ffn_b1"][n][at:at + hidden]
        w2 = np.zeros((3 * P, P), np.float32)
        w2[:hidden] = i["L2_ffn_W2"][n]
        layers.append(beside(w1[0], w1[1], in_parts(w2), b1[0].reshape(3, P).T, b1[1].reshape(3, P).T,
                             first_row(i["L2_ffn_b2"][n])))
    t["f2"] = padded(layers)
    q, k, v = (spread(i[f"L3_attn_W{c}"]) for c in "qkv")
    bq, bk, bv = (spread(i[f"L3_attn_b{c}"]) for c in "qkv")
    wo = [m.T for m in spread(i["L3_attn_Wo"].T)]
    t["a3"] = padded([beside(q[g], k[g], v[g], wo[g], column(bq[g]), column(bk[g]), on_all(bv[g])) for g in range(4)])
    t["bo3"], t["wr3"] = i["L3_attn_bo"], i["L3_ffn_Wr"].T
    t["f3"] = padded([beside(i["L3_ffn_W1"][e], in_parts(i["L3_ffn_W2"][e])) for e in range(8)])
    return {name: np.ascontiguousarray(a, dtype=np.float32) for name, a in t.items()}


def kernel(**inputs):
    from concourse import bacc
    from concourse.bass_utils import run_bass_kernel_spmd

    arrays = lay_out({name: np.asarray(a) for name, a in inputs.items()})
    nc = bacc.Bacc("TRN2", target_bir_lowering=False, num_devices=1)
    tensors = {name: nc.dram_tensor(f"in_{name}", a.shape, F32, kind="ExternalInput").ap() for name, a in arrays.items()}
    out = nc.dram_tensor("out", (BATCH, SEQ, D), F32, kind="ExternalOutput").ap()
    build(nc, tensors, out)
    results = run_bass_kernel_spmd(nc, [{f"in_{name}": a for name, a in arrays.items()}], core_ids=[0])
    return results.results[0]["out"]
```
